# Optimizing a Trainium2 kernel written in Bass

```python
import numpy as np
import jax
import jax.numpy as jnp

def _softmax(x, axis=-1):
    return jax.nn.softmax(x, axis=axis)

def _gelu(x):
    return jax.nn.gelu(x, approximate=True)

def _silu(x):
    return jax.nn.silu(x)

def _sigmoid(x):
    return jax.nn.sigmoid(x)

def _layernorm(x, axis=-1, eps=1e-05):
    m = jnp.mean(x, axis=axis, keepdims=True)
    v = jnp.var(x, axis=axis, keepdims=True)
    return (x - m) / jnp.sqrt(v + eps)

def _scatter_add(tgt, idx, src, axis=0):
    return tgt.at[idx].add(src)

def _segment_sum(src, seg, n):
    return jax.ops.segment_sum(src, seg, n)
kernel_name = 'mk_adaln_ffn_d1_seqx_r4_92a0b3'

def setup_inputs(seed: int=0):
    np.random.seed(seed)
    _w = jnp.asarray

    def _rec_inputs():
        import jax
        import jax.numpy as jnp
        _rk = jax.random.key(seed)
        x = -7.109e-05 + 0.9999 * jax.random.normal(jax.random.fold_in(_rk, 1), (2, 1024, 256), jnp.float32)
        _lenS = 1024 - jax.random.randint(jax.random.fold_in(_rk, 7), (2,), 0, max(1, 1024 // 4) + 1, jnp.int32)
        _lenS2 = 1024 - jax.random.randint(jax.random.fold_in(_rk, 8), (2,), 0, max(1, 1024 // 4) + 1, jnp.int32)
        cond_512 = 0.0061147 + 1.02565 * jax.random.normal(jax.random.fold_in(_rk, 11), (2, 128), jnp.float32)
        return (x, cond_512)
    x, cond_512 = _rec_inputs()

    def _L0_cond_setup():
        import jax, jax.numpy as jnp
        import numpy as np
        W_DIM = 128
        CLAMP = 256.0
        key = jax.random.key(seed)
        ks = jax.random.split(key, 6)
        B, L, C = (8, 2048, 256)
        return {'x': jax.random.normal(ks[0], (B, L, C), dtype=jnp.float32), 'w': jax.random.normal(ks[1], (B, W_DIM), dtype=jnp.float32), 'weight': jax.random.normal(ks[2], (C, C), dtype=jnp.float32), 'bias': jax.random.normal(ks[3], (C,), dtype=jnp.float32), 'affine_w': jax.random.normal(ks[4], (C, W_DIM), dtype=jnp.float32), 'affine_b': jnp.ones((C,), dtype=jnp.float32)}
    _L0_cond_all = _L0_cond_setup()
    _L0_cond_in = {k: v for k, v in _L0_cond_all.items() if k in ('weight', 'bias', 'affine_w', 'affine_b')}
    del _L0_cond_all

    def _L0_ffn_setup():
        import jax, jax.numpy as jnp
        import numpy as np
        E = 8
        K = 2
        D = 256
        F = 256
        B, S = (2, 512)
        key = jax.random.key(seed)
        ks = jax.random.split(key, 8)
        sc = 1.0 / np.sqrt(D)
        scf = 1.0 / np.sqrt(F)
        return {'x': jax.random.normal(ks[0], (B, S, D), dtype=jnp.float32), 'gate_w': jax.random.normal(ks[1], (D, E), dtype=jnp.float32) * sc, 'sw_gate': jax.random.normal(ks[2], (D, F), dtype=jnp.float32) * sc, 'sw_up': jax.random.normal(ks[3], (D, F), dtype=jnp.float32) * sc, 'sw_down': jax.random.normal(ks[4], (F, D), dtype=jnp.float32) * scf, 'ew_gate': jax.random.normal(ks[5], (E, D, F), dtype=jnp.float32) * sc, 'ew_up': jax.random.normal(ks[6], (E, D, F), dtype=jnp.float32) * sc, 'ew_down': jax.random.normal(ks[7], (E, F, D), dtype=jnp.float32) * scf}
    _L0_ffn_all = _L0_ffn_setup()
    _L0_ffn_in = {k: v for k, v in _L0_ffn_all.items() if k in ('gate_w', 'sw_gate', 'sw_up', 'sw_down', 'ew_gate', 'ew_up', 'ew_down')}
    del _L0_ffn_all
    return {'x': x, 'cond_512': cond_512, 'L0_cond_weight': _L0_cond_in['weight'], 'L0_cond_bias': _L0_cond_in['bias'], 'L0_cond_affine_w': _L0_cond_in['affine_w'], 'L0_cond_affine_b': _L0_cond_in['affine_b'], 'L0_ffn_gate_w': _L0_ffn_in['gate_w'], 'L0_ffn_sw_gate': _L0_ffn_in['sw_gate'], 'L0_ffn_sw_up': _L0_ffn_in['sw_up'], 'L0_ffn_sw_down': _L0_ffn_in['sw_down'], 'L0_ffn_ew_gate': _L0_ffn_in['ew_gate'], 'L0_ffn_ew_up': _L0_ffn_in['ew_up'], 'L0_ffn_ew_down': _L0_ffn_in['ew_down']}

def reference(x, cond_512, L0_cond_weight, L0_cond_bias, L0_cond_affine_w, L0_cond_affine_b, L0_ffn_gate_w, L0_ffn_sw_gate, L0_ffn_sw_up, L0_ffn_sw_down, L0_ffn_ew_gate, L0_ffn_ew_up, L0_ffn_ew_down):
    import jax
    import jax.numpy as jnp

    def _L0_cond_ref(x, w, weight, bias, affine_w, affine_b):
        import jax, jax.numpy as jnp
        import numpy as np
        W_DIM = 128
        CLAMP = 256.0
        B, L, C = x.shape
        gain = 1.0 / np.sqrt(W_DIM).astype(np.float32)
        styles = w @ (affine_w * gain).T + affine_b
        ws = weight[None, :, :] * styles[:, None, :]
        dcoefs = jax.lax.rsqrt(jnp.sum(ws * ws, axis=2) + 1e-08)
        xm = x * styles[:, None, :]
        y = jnp.einsum('blc,oc->blo', xm, weight)
        y = y * dcoefs[:, None, :]
        y = jnp.clip(y + bias, -CLAMP, CLAMP)
        return y

    def _L0_ffn_ref(x, gate_w, sw_gate, sw_up, sw_down, ew_gate, ew_up, ew_down):
        import jax, jax.numpy as jnp
        import numpy as np
        E = 8
        K = 2
        D = 256
        F = 256
        B, S = (2, 512)
        b, s, d = x.shape
        xf = x.reshape(-1, d)
        T = xf.shape[0]
        silu = jax.nn.silu
        shared = silu(xf @ sw_gate) * (xf @ sw_up) @ sw_down
        gate = jax.nn.softmax(xf @ gate_w, axis=-1)
        topw, topi = jax.lax.top_k(gate, K)
        topw = topw / (topw.sum(axis=-1, keepdims=True) + 1e-20)
        w = jnp.zeros((T, E), dtype=gate.dtype).at[jnp.arange(T)[:, None], topi].add(topw)
        h = jnp.einsum('td,edf->etf', xf, ew_gate)
        u = jnp.einsum('td,edf->etf', xf, ew_up)
        y = jnp.einsum('etf,efd->etd', silu(h) * u, ew_down)
        routed = jnp.einsum('etd,te->td', y, w)
        return (shared + routed).reshape(b, s, d)
    x = x + _L0_ffn_ref(_L0_cond_ref(x, cond_512, L0_cond_weight, L0_cond_bias, L0_cond_affine_w, L0_cond_affine_b), L0_ffn_gate_w, L0_ffn_sw_gate, L0_ffn_sw_up, L0_ffn_sw_down, L0_ffn_ew_gate, L0_ffn_ew_up, L0_ffn_ew_down)
    return x

_drawn_inputs = setup_inputs


def setup_inputs(seed=0):
    import zlib

    import numpy as np

    out = dict(_drawn_inputs(seed))
    spreads = {'L0_cond_affine_b': (1.0, 0.2)}
    factors = {}
    for name, (base, spread) in spreads.items():
        noise = np.random.default_rng([zlib.crc32(name.encode()), seed]).standard_normal(out[name].shape)
        drawn = base * np.exp(spread * noise) if base else spread * noise
        out[name] = jnp.asarray(drawn.astype(out[name].dtype))
    for name, factor in factors.items():
        out[name] = (out[name] * factor).astype(out[name].dtype)
    return out
```

```python
from contextlib import ExitStack

import concourse.bass as bass
from concourse import mybir

P = 128
F32 = mybir.dt.float32
F32R = mybir.dt.float32r
BF16 = mybir.dt.bfloat16
I32 = mybir.dt.int32
U32 = mybir.dt.uint32
ALU = mybir.AluOpType
ACT = mybir.ActivationFunctionType
AX_X = mybir.AxisListType.X

CLAMP = 256.0
STYLE_DIM = 128
GAIN = float(STYLE_DIM) ** -0.5
DEMOD_EPS = 1e-8
TOPW_EPS = 1e-20
TOP = 2
OUT_OF_RANGE = float(1 << 20)


def adaln_moe_ffn(nc, xT, x_rows, small, bias, ffn_w, out, batches, n_experts):
    T, C = x_rows.shape
    KC = C // P
    F = C
    FFN_W = 2 * F + C
    E = n_experts
    NF = E + 1
    TILES = T // P
    RING = 4
    PAIRS = TOP * TILES
    ROUTED = PAIRS + E - 1
    SLOTS = ROUTED + 1
    FRONT = 9
    STEPS = TILES + ROUTED
    R = 3
    LOOP = (FRONT + R, FRONT + ROUTED - R)
    assert FRONT % R == 0 and ROUTED % R == 0 and KC == 2 and TILES % RING == 0

    at, col = 0, {}
    for name, n in (("affT", C), ("condT", batches), ("affb", KC), ("WT", KC * C), ("gate", KC * E)):
        col[name] = slice(at, at + n)
        at += n
    SMALL = at

    y_rows = nc.dram_tensor("y_rows", (T, C), F32).ap()
    z_rows = nc.dram_tensor("z_rows", (TOP * T, C), F32).ap()

    with ExitStack() as ctx:
        def sb(name, shape, dt=F32):
            return ctx.enter_context(nc.sbuf_tensor(name, shape, dt))

        def psum(name, shape, dt=F32):
            return ctx.enter_context(nc.psum_tensor(name, shape, dt))

        def sem(name):
            return ctx.enter_context(nc.semaphore(name))

        def sems(name, n):
            return [sem(f"{name}{i}") for i in range(n)]

        w_hi = sb("w_hi", [P, NF, KC, FFN_W], F32R)
        w_lo = sb("w_lo", [P, NF, KC, FFN_W], F32R)
        w_raw = sb("w_raw", [P, 2, KC, FFN_W])
        base = sb("base", [P, TILES, C])
        small_sb = sb("small_sb", [P, SMALL])
        bias_bc = sb("bias_bc", [P, C])
        demod_bc = sb("demod_bc", [P, batches, C])
        ws_raw = sb("ws_raw", [P, 2 * KC * batches * C])
        ws_hi = sb("ws_hi", [P, KC, batches, C], F32R)
        ws_lo = sb("ws_lo", [P, KC, batches, C], F32R)
        gate_s = sb("gate_s", [P, 2, KC, E], F32R)
        x_split = sb("x_split", [P, 2, RING, KC, P], F32R)
        y_row = sb("y_row", [P, RING, C])
        yT = sb("yT", [P, 2, RING, KC, P], F32R)
        x_in_sb = sb("x_in_sb", [P, R, C])
        ident = sb("ident", [P, P])
        ones = sb("ones", [P, P])
        styles = sb("styles", [P, KC, batches])
        dem = sb("dem", [P, 4, KC, batches])
        diag = sb("diag", [P, KC, batches, P])

        ws = ws_raw[:, 0:KC * batches * C].rearrange("p (k b o) -> p k b o", k=KC, b=batches)
        x_raw = ws_raw[:, KC * batches * C:2 * KC * batches * C].rearrange("p (r k t) -> p r k t", r=RING, k=KC)
        hidden = ws_raw[:, 0:2 * R * F].rearrange("p (a r f) -> p a r f", a=2, r=R)
        aT = x_split[:, 1, 0:2, :, :]
        xT_s0 = x_split[:, 0, 0:2, :, :]
        xT_s1 = x_split[:, 0, 2:4, :, :]
        xT_s2 = x_split[:, 1, 2:4, :, :]
        xT_s = [xT_s0, xT_s1, xT_s2]
        z_sb = y_row[:, 0:R, :]
        ZR = 6
        z_in = w_raw[:, :, :, :].rearrange("p a k n -> p (a k n)")[:, 0:ZR * TOP * C].rearrange(
            "p (n c m) -> p n c m", n=ZR, c=TOP)

        rank = sb("rank", [P, TILES, E])
        prob = sb("prob", [P, TILES, E])
        tmp = sb("tmp", [P, TILES, E])
        hit = sb("hit", [P, TOP, TILES, E])
        posh = sb("posh", [P, TOP, TILES, E])
        stat = sb("stat", [P, 8, TILES])
        member = sb("member", [P, TILES, E], BF16)
        below = sb("below", [P, P], BF16)
        ones_b = sb("ones_b", [P, P], BF16)
        PADT = TILES // 2
        scan = sb("scan", [P, 2, PADT + TILES, E])
        tiles_i = sb("tiles_i", [P, E], I32)
        escan = sb("escan", [P, 3, E // 2 + E])
        pos = sb("pos", [P, PAIRS])
        pos_i = sb("pos_i", [P, 3, PAIRS], I32)
        pos_lo = sb("pos_lo", [P, PAIRS])
        pos_hi = sb("pos_hi", [P, PAIRS], BF16)
        iota_row = sb("iota_row", [P, P], BF16)
        iota_slot = sb("iota_slot", [P, SLOTS], BF16)
        iota_slot_f = sb("iota_slot_f", [P, SLOTS])
        iota_pair = sb("iota_pair", [P, PAIRS], BF16)
        part = sb("part", [P, 1])
        one_lo = sb("one_lo", [P, PAIRS, P], BF16)
        one_hi = sb("one_hi", [P, PAIRS, SLOTS], BF16)
        pay = base[:, TILES // 2:, :].rearrange("p t c -> p (t c)").bitcast(BF16)[:, 0:3 * PAIRS * SLOTS].rearrange(
            "p (a q s) -> p a q s", a=3, q=PAIRS)
        w_pair = sb("w_pair", [P, 3, PAIRS])
        w_bits = sb("w_bits", [P, 3, PAIRS], BF16)
        slot_f = sb("slot_f", [P, 4, SLOTS])
        slot_g = sb("slot_g", [P, SLOTS], U32)
        slot_s = sb("slot_s", [P, SLOTS], U32)
        slot_w = sb("slot_w", [P, SLOTS])
        emap_c = sb("emap_c", [P, SLOTS, E])
        emap_f = sb("emap_f", [P, SLOTS])
        emap = sb("emap", [P, SLOTS], I32)

        gu = [psum(f"gu{i}", [P, 2 * F]) for i in range(R)]
        t1_ps = psum("t1_ps", [P, KC, P])
        t2_ps = psum("t2_ps", [P, KC, P])
        z_ps = psum("z_ps", [P, C])
        logit_ps = psum("logit_ps", [P, TILES, E])
        misc_ps = psum("misc_ps", [P, 512])
        style_ps = misc_ps[:, 0:KC * batches].rearrange("p (k b) -> p k b", k=KC)
        dem_ps = misc_ps[:, 8:8 + KC * batches].rearrange("p (k b) -> p k b", k=KC)
        before_ps = misc_ps[:, 0:TILES * E].rearrange("p (t e) -> p t e", t=TILES)
        total_ps = misc_ps[:, TILES * E:2 * TILES * E].rearrange("p (t e) -> p t e", t=TILES)
        inv_ps = logit_ps[:, :, :].rearrange("p t e -> p (t e)")
        slot_id_ps = misc_ps[:, 0:2 * SLOTS].rearrange("p (a s) -> p a s", a=2)
        slot_w_ps = misc_ps[:, 2 * SLOTS:5 * SLOTS].rearrange("p (a s) -> p a s", a=3)
        cond_ps = [gu[0][:, 0:C], gu[1][:, 0:C]]
        yT_ps = [t1_ps, t2_ps]
        demod_ps = gu[2][:, :].rearrange("p (b o) -> p b o", b=batches)

        small_in = sem("small_in")
        bias_in = sem("bias_in")
        xT_in = sems("xT_in", RING)
        w_in = sems("w_in", 2)
        base_in = sems("base_in", 2)
        consts = sem("consts")
        iotas = sem("iotas")
        style_mm = sem("style_mm")
        dve_prep = sem("dve_prep")
        wsq_done = sem("wsq_done")
        dem_mm = sem("dem_mm")
        dem_sqrt = sem("dem_sqrt")
        diag_done = sem("diag_done")
        demod_mm = sem("demod_mm")
        demod_done = sem("demod_done")
        ws_split = sem("ws_split")
        x_hi_done = sem("x_hi_done")
        x_lo_done = sem("x_lo_done")
        cond_mm = sem("cond_mm")
        y_scaled = sem("y_scaled")
        y_biased = sem("y_biased")
        y_done = sem("y_done")
        y_stored = sems("y_stored", RING)
        yT_mm = sem("yT_mm")
        yT_hi_done = sem("yT_hi_done")
        yT_lo_done = sem("yT_lo_done")
        logit_mm = sem("logit_mm")
        w_hi_done = sem("w_hi_done")
        w_lo_done = sem("w_lo_done")
        rt = sem("rt")
        exp_ready = sem("exp_ready")
        exp_done = sem("exp_done")
        member_done = sem("member_done")
        before_mm = sem("before_mm")
        one_lo_done = sem("one_lo_done")
        id_pay_done = sem("id_pay_done")
        id_mm = sem("id_mm")
        w_pay_done = sem("w_pay_done")
        w_mm = sem("w_mm")
        slots_done = sem("slots_done")
        slot_w_done = sem("slot_w_done")
        emap_done = sem("emap_done")
        rows_in = sems("rows_in", R)
        gathered = sems("gathered", R)
        t1_mm = sem("t1_mm")
        xT_hi_done = sem("xT_hi_done")
        xT_lo_done = sem("xT_lo_done")
        gu_mm = sem("gu_mm")
        silu_done = sem("silu_done")
        product_done = sem("product_done")
        t2_mm = sem("t2_mm")
        aT_hi_done = sem("aT_hi_done")
        aT_lo_done = sem("aT_lo_done")
        down_mm = sem("down_mm")
        z_read = sem("z_read")
        z_out = sems("z_out", R)
        z_back = sems("z_back", ZR)
        fin1 = sem("fin1")
        fin2 = sem("fin2")
        stored = sem("stored")

        f32 = lambda ap: ap.bitcast(F32)
        affT, condT, affb = (small_sb[:, col[n]] for n in ("affT", "condT", "affb"))
        WT = small_sb[:, col["WT"]].rearrange("p (k o) -> p k o", k=KC)
        gate_w = small_sb[:, col["gate"]].rearrange("p (k e) -> p k e", k=KC)
        x_rows_v = x_rows.rearrange("(n p) c -> p n c", p=P)
        out_v = out.rearrange("(n p) c -> p n c", p=P)
        y_v = y_rows.rearrange("(n p) c -> p n c", p=P)
        z_v = z_rows.rearrange("(a n p) c -> p n a c", p=P, a=TOP)

        def routed(n):
            return not isinstance(n, int) or FRONT <= n < FRONT + ROUTED

        def shared_tile(n):
            return n if n < FRONT else n - ROUTED

        def slot_tile(n):
            return n - FRONT

        def walk(eng, iteration, start=0):
            for n in range(start, LOOP[0]):
                iteration(n, n % R, n // R)
            with eng.Fori(LOOP[0] // R, LOOP[1] // R) as turn:
                for j in range(R):
                    iteration(turn * R + j, j, turn)
            for n in range(LOOP[1], STEPS):
                iteration(n, n % R, n // R)

        def is_step(n):
            return not isinstance(n, int) or n < STEPS

        def walk_tiles(eng, tile_step):
            for n in range(RING):
                tile_step(n, n, 0)
            with eng.Fori(1, TILES // RING) as lap:
                for j in range(RING):
                    tile_step(lap * RING + j, j, lap)

        def lag(n, slot, by):
            if isinstance(n, int) and n < by:
                return None, None
            return n - by, (slot - by) % RING

        block = ctx.enter_context(nc.Block())

        @block.sync
        def _(sp):
            def load_x(n):
                if n >= RING:
                    sp.wait_ge(x_hi_done, n - RING + 1)
                    sp.wait_ge(x_lo_done, n - RING + 1)
                sp.dma_start(x_raw[:, n % RING, :, :], xT[n]).then_inc(xT_in[n % RING], 16)

            def load_w(f):
                if f >= 2:
                    sp.wait_ge(w_hi_done, f - 1)
                    sp.wait_ge(w_lo_done, f - 1)
                sp.dma_start(w_raw[:, f % 2, :, :], ffn_w[f]).then_inc(w_in[f % 2], 16)

            def store_y(n):
                sp.wait_ge(y_done, n + 1)
                sp.dma_start(y_v[:, n, :], y_row[:, n % RING, :]).then_inc(y_stored[n % RING], 16)

            def load_rows(n):
                if n >= R:
                    sp.wait_ge(t1_mm, n - R + 1)
                t = shared_tile(n)
                sp.wait_ge(y_stored[t % RING], 16 * (t // RING + 1))
                sp.dma_start(x_in_sb[:, n % R, :], y_v[:, t, :]).then_inc(rows_in[n % R], 16)

            sp.dma_start(small_sb[:, :], small).then_inc(small_in, 16)
            for n in range(RING):
                load_x(n)
            sp.dma_start(bias_bc[:, :], bias.rearrange("(o c) -> o c", o=1).broadcast_to([P, C])).then_inc(bias_in, 16)
            load_w(0)
            load_w(1)
            for n in range(RING, TILES):
                load_x(n)
                store_y(n - RING)
                if n == 8:
                    sp.wait_ge(dem_mm, 1)
                    sp.dma_start(base[:, 0:TILES // 2, :], x_rows_v[:, 0:TILES // 2, :]).then_inc(base_in[0], 16)
                if n in (9, 13):
                    load_w(2 + (n - 9) // 4)
            for n in range(R):
                load_rows(n)
            for n in range(TILES - RING, TILES):
                store_y(n)
            for n in range(R, FRONT):
                if n < 8:
                    load_w(n + 1)
                load_rows(n)
            sp.wait_ge(w_mm, 1)
            sp.dma_start(base[:, TILES // 2:, :], x_rows_v[:, TILES // 2:, :]).then_inc(base_in[1], 16)
            for n in range(FRONT + ROUTED, STEPS):
                load_rows(n)
            for slot in range(R):
                sp.wait_ge(z_out[slot], 16 * (ROUTED // R))

            def load_z(t):
                if t >= ZR:
                    sp.wait_ge(fin2, t - ZR + 1)
                sp.dma_start(z_in[:, t % ZR, :, :], z_v[:, t, :, :]).then_inc(z_back[t % ZR], 16)

            def store(t):
                sp.wait_ge(fin2, t + 1)
                sp.dma_start(out_v[:, t, :], base[:, t, :]).then_inc(stored, 16)

            for t in range(ZR):
                load_z(t)
            for t in range(TILES):
                store(t)
                if t + ZR < TILES:
                    load_z(t + ZR)
            sp.wait_ge(stored, 16 * TILES)

        @block.gpsimd
        def _(pool):
            pool.memset(ones[:, :], 1.0)
            pool.memset(ident[:, :], 0.0).then_inc(consts, 1)
            pool.wait_ge(consts, 1)
            pool.affine_select(out=ident[:, :], in_=ident[:, :], compare_op=ALU.not_equal, fill=1.0,
                               base=0, pattern=[[-1, P]], channel_multiplier=1).then_inc(consts, 1)
            pool.wait_ge(dve_prep, 1 + KC * batches)
            pool.tensor_tensor(base[:, 0:4, :].rearrange("p a c -> p (a c)"),
                               ws_raw[:, 0:KC * batches * C], ws_raw[:, 0:KC * batches * C],
                               ALU.mult).then_inc(wsq_done, 1)

            def split_w(f):
                pool.wait_ge(w_in[f % 2], 16 * (f // 2 + 1))
                pool.wait_ge(w_hi_done, f + 1)
                pool.tensor_tensor(w_lo[:, f, :, :], w_raw[:, f % 2, :, :], f32(w_hi[:, f, :, :]),
                                   ALU.subtract).then_inc(w_lo_done, 1)

            def x_lo(n):
                pool.wait_ge(xT_in[n % RING], 16 * (n // RING + 1))
                pool.wait_ge(x_hi_done, n + 1)
                pool.tensor_tensor(x_split[:, 1, n % RING, :, :], x_raw[:, n % RING, :, :],
                                   f32(x_split[:, 0, n % RING, :, :]), ALU.subtract).then_inc(x_lo_done, 1)

            for n in range(TILES):
                x_lo(n)
                if n == 3:
                    for e in range(E):
                        pool.memset(rank[:, :, e:e + 1], float(E - e))
                    pool.memset(ones_b[:, :], 1.0)
                    pool.memset(scan[:, :, :, :], 0.0)
                    pool.memset(escan[:, :, :], 0.0).then_inc(iotas, 1)
                if n == 5:
                    split_w(0)
                if n == 8:
                    pool.affine_select(out=below[:, :], in_=ones_b[:, :], compare_op=ALU.is_gt, fill=0.0,
                                       base=0, pattern=[[1, P]], channel_multiplier=-1)
                    pool.iota(iota_row[:, :], [[1, P]], base=0, channel_multiplier=0,
                              allow_small_or_imprecise_dtypes=True)
                    pool.iota(iota_slot[:, :], [[1, SLOTS]], base=0, channel_multiplier=0,
                              allow_small_or_imprecise_dtypes=True)
                    pool.iota(iota_slot_f[:, :], [[1, SLOTS]], base=0, channel_multiplier=0,
                              allow_small_or_imprecise_dtypes=True)
                    pool.iota(iota_pair[:, :], [[1, PAIRS]], base=1, channel_multiplier=0,
                              allow_small_or_imprecise_dtypes=True)
                    pool.iota(part[:, :], [[0, 1]], base=0, channel_multiplier=1,
                              allow_small_or_imprecise_dtypes=True).then_inc(iotas, 1)
                if n == 11:
                    split_w(1)
            for f in range(2, NF):
                split_w(f)

            def gather(n):
                pool.wait_ge(t1_mm, n - R + 1)
                r = slot_tile(n)
                pool.indirect_dma_start(x_in_sb[:, n % R, :], None, y_rows,
                                        bass.IndirectOffsetOnAxis(ap=slot_g[:, r:r + 1], axis=0)
                                        ).then_inc(gathered[n % R], 16)

            def scatter(n):
                pool.wait_ge(z_read, n + 1)
                r = slot_tile(n)
                pool.indirect_dma_start(z_rows, bass.IndirectOffsetOnAxis(ap=slot_s[:, r:r + 1], axis=0),
                                        z_sb[:, n % R, :], None, bounds_check=TOP * T - 1,
                                        oob_is_err=False).then_inc(z_out[n % R], 16)

            pool.wait_ge(slots_done, 1)
            for slot in range(RING):
                pool.wait_ge(y_stored[slot], 16 * (TILES // RING))
            for n in range(FRONT, FRONT + 2 * R):
                gather(n)
            for n in range(FRONT, FRONT + ROUTED):
                if n + 2 * R < FRONT + ROUTED:
                    gather(n + 2 * R)
                scatter(n)

        @block.scalar
        def _(act):
            def split_w(f):
                act.wait_ge(w_in[f % 2], 16 * (f // 2 + 1))
                act.copy(w_hi[:, f, :, :], w_raw[:, f % 2, :, :]).then_inc(w_hi_done, 1)

            def x_hi(n):
                act.wait_ge(xT_in[n % RING], 16 * (n // RING + 1))
                if n >= RING:
                    act.wait_ge(cond_mm, n - RING + 1)
                act.copy(x_split[:, 0, n % RING, :, :], x_raw[:, n % RING, :, :]).then_inc(x_hi_done, 1)

            def yT_hi(n):
                act.wait_ge(yT_mm, n + 1)
                if n >= RING:
                    act.wait_ge(logit_mm, n - RING + 1)
                act.copy(yT[:, 0, n % RING, :, :], yT_ps[n % 2][:, :, :]).then_inc(yT_hi_done, 1)

            for n in range(RING):
                x_hi(n)
            act.wait_ge(dve_prep, 2 + KC * batches)
            act.activation(dem[:, 1, :, :], dem[:, 0, :, :], ACT.Sqrt).then_inc(dem_sqrt, 1)
            act.wait_ge(demod_mm, 1)
            act.copy(demod_bc[:, :, :], demod_ps[:, :, :]).then_inc(demod_done, 1)
            for n in range(TILES):
                if n + RING < TILES:
                    x_hi(n + RING)
                yT_hi(n)
                if n in (1, 3):
                    split_w(n // 2)
                if n in (9, 13):
                    split_w(2 + (n - 9) // 4)
            act.wait_ge(exp_ready, 1)
            act.activation(prob[:, :, :], tmp[:, :, :], ACT.Exp).then_inc(exp_done, 1)

            def xT_hi(n, slot):
                act.wait_ge(t1_mm, n + 1)
                if not isinstance(n, int) or n >= R:
                    act.wait_ge(gu_mm, n - R + 1)
                act.copy(xT_s[slot][:, 0, :, :], t1_ps[:, :, :]).then_inc(xT_hi_done, 1)

            def silu(n, slot):
                act.wait_ge(gu_mm, n + 1)
                if not isinstance(n, int) or n >= R:
                    act.wait_ge(product_done, n - R + 1)
                act.activation(hidden[:, 0, slot, :], gu[slot][:, 0:F], ACT.Silu).then_inc(silu_done, 1)

            def aT_hi(n):
                act.wait_ge(t2_mm, n + 1)
                act.copy(aT[:, 0, :, :], t2_ps[:, :, :]).then_inc(aT_hi_done, 1)

            def read_z(n, slot, turn):
                act.wait_ge(down_mm, n + 1)
                if not isinstance(n, int) or n >= FRONT + R:
                    act.wait_ge(z_out[slot], (turn - FRONT // R) * 16)
                act.copy(z_sb[:, slot, :], z_ps[:, :]).then_inc(z_read, 1)

            def iteration(n, slot, turn):
                aT_hi(n)
                if is_step(n + 3):
                    xT_hi(n + 3, slot)
                if is_step(n + 2):
                    silu(n + 2, (slot + 2) % R)
                if routed(n):
                    read_z(n, slot, turn)
                if isinstance(n, int) and n < 5:
                    split_w(n + 4)

            for n in range(3):
                xT_hi(n, n)
            silu(0, 0)
            silu(1, 1)
            walk(act, iteration)

        @block.vector
        def _(dve):
            dve.wait_ge(small_in, 16)
            dve.wait_ge(style_mm, 1)
            for k in range(KC):
                ins = dve.tensor_scalar(styles[:, k, :], style_ps[:, k, :], GAIN, affb[:, k:k + 1],
                                        ALU.mult, ALU.add)
            ins.then_inc(dve_prep, 1)
            dve.wait_ge(dve_prep, 1)
            for k in range(KC):
                for b in range(batches):
                    dve.tensor_scalar(ws[:, k, b, :], WT[:, k, :], styles[:, k, b:b + 1], None,
                                      ALU.mult).then_inc(dve_prep, 1)
            dve.tensor_copy(gate_s[:, 0, :, :], gate_w).then_inc(ws_split, 1)
            dve.wait_ge(dve_prep, 1 + KC * batches)
            dve.tensor_copy(ws_hi[:, :, :, :], ws[:, :, :, :]).then_inc(ws_split, 1)
            dve.wait_ge(ws_split, 2)
            dve.tensor_tensor(ws_lo[:, :, :, :], ws[:, :, :, :], f32(ws_hi[:, :, :, :]),
                              ALU.subtract).then_inc(ws_split, 1)
            dve.tensor_tensor(gate_s[:, 1, :, :], gate_w, f32(gate_s[:, 0, :, :]),
                              ALU.subtract).then_inc(ws_split, 1)
            v, root, r, c = (dem[:, i, :, :] for i in range(4))
            dve.wait_ge(dem_mm, 1)
            dve.tensor_scalar(v, dem_ps[:, :, :], DEMOD_EPS, None, ALU.add).then_inc(dve_prep, 1)
            step = 3 + KC * batches
            dve.wait_ge(dem_sqrt, 1)
            dve.reciprocal(r, root).then_inc(dve_prep, 1)
            dve.wait_ge(dve_prep, step)
            dve.tensor_tensor(c, r, r, ALU.mult).then_inc(dve_prep, 1)
            dve.wait_ge(dve_prep, step + 1)
            dve.tensor_tensor(c, c, v, ALU.mult).then_inc(dve_prep, 1)
            dve.wait_ge(dve_prep, step + 2)
            dve.tensor_scalar(c, c, -0.5, 1.5, ALU.mult, ALU.add).then_inc(dve_prep, 1)
            dve.wait_ge(dve_prep, step + 3)
            dve.tensor_tensor(r, r, c, ALU.mult).then_inc(dve_prep, 1)
            dve.wait_ge(dve_prep, step + 4)
            dve.wait_ge(consts, 2)
            for k in range(KC):
                for b in range(batches):
                    ins = dve.tensor_scalar(diag[:, k, b, :], ident[:, :], dem[:, 2, k, b:b + 1], None, ALU.mult)
            ins.then_inc(diag_done, 1)

            def scale_y(n, slot, lap):
                first = isinstance(n, int) and n < RING
                dve.wait_ge(cond_mm, n + 1)
                if not first:
                    dve.wait_ge(y_stored[slot], lap * 16)
                    dve.wait_ge(yT_mm, n - RING + 1)
                tiles_per_batch = TILES // batches
                bb = n // tiles_per_batch if isinstance(n, int) else lap // (tiles_per_batch // RING)
                dve.tensor_tensor(y_row[:, slot, :].rearrange("p (o c) -> p o c", o=1), cond_ps[slot % 2].rearrange("p (o c) -> p o c", o=1),
                                  demod_bc[:, bass.ds(bb, 1), :], ALU.mult).then_inc(y_scaled, 1)

            def bias_y(n, slot):
                dve.wait_ge(y_scaled, n + 1)
                dve.tensor_tensor(y_row[:, slot, :], y_row[:, slot, :], bias_bc[:, :], ALU.add).then_inc(y_biased, 1)

            def clip_y(n, slot):
                dve.wait_ge(y_biased, n + 1)
                dve.tensor_scalar(y_row[:, slot, :], y_row[:, slot, :], CLAMP, -CLAMP,
                                  ALU.min, ALU.max).then_inc(y_done, 1)

            def yT_lo(n, slot):
                dve.wait_ge(yT_hi_done, n + 1)
                dve.tensor_tensor(yT[:, 1, slot, :, :], yT_ps[slot % 2][:, :, :], f32(yT[:, 0, slot, :, :]),
                                  ALU.subtract).then_inc(yT_lo_done, 1)

            def tile_step(n, slot, lap):
                scale_y(n, slot, lap)
                bias_y(n, slot)
                clip_y(n, slot)
                m, s = lag(n, slot, 3)
                if m is not None:
                    yT_lo(m, s)

            dve.wait_ge(bias_in, 16)
            dve.wait_ge(demod_done, 1)
            walk_tiles(dve, tile_step)
            for n in range(TILES - 3, TILES):
                yT_lo(n, n % RING)

            count = [0]

            def link(ins):
                count[0] += 1
                ins.then_inc(rt, 1)
                dve.wait_ge(rt, count[0])

            bc = lambda s: s.unsqueeze(2).broadcast_to([P, TILES, E])
            mx, total, rtotal, top1, top2, key, rsum = (stat[:, i, :] for i in range(7))

            def logits_less_max():
                dve.wait_ge(logit_mm, TILES)
                link(dve.tensor_reduce(mx, logit_ps[:, :, :], AX_X, ALU.max))
                dve.tensor_tensor(tmp[:, :, :], logit_ps[:, :, :], bc(mx), ALU.subtract).then_inc(exp_ready, 1)

            def softmax():
                dve.wait_ge(exp_done, 1)
                link(dve.tensor_reduce(total, prob[:, :, :], AX_X, ALU.add))
                link(dve.reciprocal(rtotal, total))
                link(dve.tensor_tensor(prob[:, :, :], prob[:, :, :], bc(rtotal), ALU.mult))

            def pick(n, top):
                h = hit[:, n, :, :]
                link(dve.tensor_reduce(top, prob[:, :, :], AX_X, ALU.max))
                link(dve.tensor_tensor(h, prob[:, :, :], bc(top), ALU.is_equal))
                link(dve.tensor_tensor(h, h, rank[:, :, :], ALU.mult))
                link(dve.tensor_reduce(key, h, AX_X, ALU.max))
                link(dve.tensor_tensor(h, h, bc(key), ALU.is_equal))

            def take_top_out():
                link(dve.scalar_tensor_tensor(out=prob[:, :, :], in0=hit[:, 0, :, :], scalar=-2.0,
                                              in1=prob[:, :, :], op0=ALU.mult, op1=ALU.add))

            def members():
                dve.tensor_tensor(member[:, :, :], hit[:, 0, :, :], hit[:, 1, :, :], ALU.add).then_inc(member_done, 1)

            def pair_weights():
                link(dve.tensor_tensor(rsum, top1, top2, ALU.add))
                link(dve.tensor_scalar(rsum, rsum, TOPW_EPS, None, ALU.add))
                link(dve.reciprocal(rsum, rsum))
                link(dve.tensor_tensor(w_pair[:, 0, 0:TILES], top1, rsum, ALU.mult))
                link(dve.tensor_tensor(w_pair[:, 0, TILES:PAIRS], top2, rsum, ALU.mult))
                for i in range(3):
                    link(dve.tensor_copy(w_bits[:, i, :], w_pair[:, i, :]))
                    if i < 2:
                        link(dve.tensor_tensor(w_pair[:, i + 1, :], w_pair[:, i, :], w_bits[:, i, :], ALU.subtract))

            def positions():
                dve.wait_ge(before_mm, 1)
                link(dve.tensor_copy(scan[:, 0, PADT:, :], total_ps[:, :, :]))
                src = 0
                for d in (1, 2, 4, 8):
                    link(dve.tensor_tensor(scan[:, 1 - src, PADT:, :], scan[:, src, PADT:, :],
                                           scan[:, src, PADT - d:PADT + TILES - d, :], ALU.add))
                    src = 1 - src
                last = scan[:, src, PADT + TILES - 1, :]
                link(dve.tensor_scalar(tiles_i[:, :], last, float(P - 1), None, ALU.add))
                link(dve.tensor_scalar(tiles_i[:, :], tiles_i[:, :], 7, None, ALU.logical_shift_right))
                H = E // 2
                link(dve.tensor_copy(escan[:, 0, H:], tiles_i[:, :]))
                es = 0
                for d in (1, 2, 4):
                    link(dve.tensor_tensor(escan[:, 1 - es, H:], escan[:, es, H:], escan[:, es, H - d:H + E - d], ALU.add))
                    es = 1 - es
                link(dve.tensor_tensor(escan[:, 2, H:], escan[:, es, H:], tiles_i[:, :], ALU.subtract))
                link(dve.tensor_scalar(escan[:, 2, H:], escan[:, 2, H:], float(P), None, ALU.mult))
                link(dve.tensor_tensor(tmp[:, :, :], scan[:, src, PADT:, :], total_ps[:, :, :], ALU.subtract))
                link(dve.tensor_tensor(tmp[:, :, :], tmp[:, :, :], before_ps[:, :, :], ALU.add))
                link(dve.tensor_tensor(tmp[:, :, :], tmp[:, :, :],
                                       escan[:, 2, H:].unsqueeze(1).broadcast_to([P, TILES, E]), ALU.add))
                for a in range(TOP):
                    link(dve.tensor_tensor(posh[:, a, :, :], hit[:, a, :, :], tmp[:, :, :], ALU.mult))
                link(dve.tensor_reduce(pos[:, :], posh[:, :, :, :].rearrange("p a t e -> p (a t) e"), AX_X, ALU.add))
                link(dve.tensor_copy(pos_i[:, 0, :], pos[:, :]))
                link(dve.tensor_scalar(pos_i[:, 1, :], pos_i[:, 0, :], P - 1, None, ALU.bitwise_and))
                link(dve.tensor_scalar(pos_i[:, 2, :], pos_i[:, 0, :], 7, None, ALU.logical_shift_right))
                link(dve.tensor_copy(pos_lo[:, :], pos_i[:, 1, :]))
                link(dve.tensor_copy(pos_hi[:, :], pos_i[:, 2, :]))
                return es

            def expert_map(es):
                H = E // 2
                link(dve.tensor_tensor(emap_c[:, :, :], iota_slot_f[:, :].unsqueeze(2).broadcast_to([P, SLOTS, E]),
                                       escan[:, es, H:].unsqueeze(1).broadcast_to([P, SLOTS, E]), ALU.is_ge))
                link(dve.tensor_reduce(emap_f[:, :], emap_c[:, :, :], AX_X, ALU.add))
                dve.tensor_scalar(emap[:, :], emap_f[:, :], float(E - 1), 1.0, ALU.min, ALU.add).then_inc(emap_done, 1)

            def one_hot_rows(a, b):
                for q in range(a, b):
                    ins = dve.tensor_scalar(one_lo[:, q, :], iota_row[:, :], pos_lo[:, q:q + 1], None, ALU.is_equal)
                ins.then_inc(one_lo_done, 1)

            def one_hot_tiles():
                link(dve.tensor_tensor(one_hi[:, :, :], iota_slot[:, :].unsqueeze(1).broadcast_to([P, PAIRS, SLOTS]),
                                       pos_hi[:, :].unsqueeze(2).broadcast_to([P, PAIRS, SLOTS]), ALU.is_equal))
                dve.tensor_tensor(pay[:, 0, :, :], one_hi[:, :, :],
                                  iota_pair[:, :].unsqueeze(2).broadcast_to([P, PAIRS, SLOTS]), ALU.mult).then_inc(id_pay_done, 1)
                dve.tensor_scalar(pay[:, 1, :, :], one_hi[:, :, :], part[:, 0:1], None, ALU.mult).then_inc(id_pay_done, 1)

            def weight_payload():
                dve.wait_ge(id_mm, 1)
                for i in range(3):
                    dve.tensor_tensor(pay[:, i, :, :], one_hi[:, :, :],
                                      w_bits[:, i, :].unsqueeze(2).broadcast_to([P, PAIRS, SLOTS]), ALU.mult).then_inc(w_pay_done, 1)

            def slot_indices():
                dve.wait_ge(id_mm, 1)
                link(dve.tensor_copy(slot_f[:, 1, :], slot_id_ps[:, 1, :]))
                link(dve.scalar_tensor_tensor(out=slot_f[:, 0, :], in0=slot_id_ps[:, 0, :], scalar=float(P),
                                              in1=slot_f[:, 1, :], op0=ALU.mult, op1=ALU.add))
                link(dve.tensor_scalar(slot_f[:, 2, :], slot_f[:, 0, :], float(T + P), float(-T), ALU.is_ge, ALU.mult))
                link(dve.scalar_tensor_tensor(out=slot_f[:, 2, :], in0=slot_f[:, 0, :], scalar=float(-P),
                                              in1=slot_f[:, 2, :], op0=ALU.add, op1=ALU.add))
                link(dve.tensor_scalar(slot_g[:, :], slot_f[:, 2, :], 0.0, None, ALU.max))
                link(dve.tensor_scalar(slot_f[:, 3, :], slot_f[:, 0, :], float(P), OUT_OF_RANGE, ALU.is_lt, ALU.mult))
                link(dve.tensor_scalar(slot_f[:, 0, :], slot_f[:, 0, :], float(-P), None, ALU.add))
                link(dve.tensor_tensor(slot_s[:, :], slot_f[:, 0, :], slot_f[:, 3, :], ALU.add))
                dve.tensor_copy(slot_f[:, 1, :], slot_f[:, 0, :]).then_inc(slots_done, 1)

            def slot_weights():
                dve.wait_ge(w_mm, 1)
                link(dve.tensor_copy(slot_w[:, :], slot_w_ps[:, 0, :]))
                link(dve.tensor_tensor(slot_w[:, :], slot_w[:, :], slot_w_ps[:, 1, :], ALU.add))
                link(dve.tensor_tensor(slot_w[:, :], slot_w[:, :], slot_w_ps[:, 2, :], ALU.add))

            def xT_lo(n, slot):
                dve.wait_ge(xT_hi_done, n + 1)
                dve.tensor_tensor(xT_s[slot][:, 1, :, :], t1_ps[:, :, :], f32(xT_s[slot][:, 0, :, :]),
                                  ALU.subtract).then_inc(xT_lo_done, 1)

            def product(n, slot):
                dve.wait_ge(silu_done, n + 1)
                w = slot_w[:, bass.ds(slot_tile(n), 1)] if routed(n) else ones[:, 0:1]
                dve.scalar_tensor_tensor(out=hidden[:, 1, slot, :], in0=gu[slot][:, F:2 * F], scalar=w,
                                         in1=hidden[:, 0, slot, :], op0=ALU.mult, op1=ALU.mult).then_inc(product_done, 1)

            def aT_lo(n):
                dve.wait_ge(aT_hi_done, n + 1)
                dve.tensor_tensor(aT[:, 1, :, :], t2_ps[:, :, :], f32(aT[:, 0, :, :]),
                                  ALU.subtract).then_inc(aT_lo_done, 1)

            def add_shared(n):
                t = shared_tile(n)
                dve.wait_ge(down_mm, n + 1)
                dve.wait_ge(base_in[t // (TILES // 2)], 16)
                dve.tensor_tensor(base[:, t, :], z_ps[:, :], base[:, t, :], ALU.add).then_inc(z_read, 1)

            def add_choices(t):
                dve.wait_ge(z_back[t % ZR], 16 * (t // ZR + 1))
                if t >= FRONT:
                    dve.wait_ge(z_read, FRONT + ROUTED + t - FRONT + 1)
                dve.tensor_tensor(base[:, t, :], base[:, t, :], z_in[:, t % ZR, 0, :], ALU.add).then_inc(fin1, 1)
                dve.wait_ge(fin1, t + 1)
                dve.tensor_tensor(base[:, t, :], base[:, t, :], z_in[:, t % ZR, 1, :], ALU.add).then_inc(fin2, 1)

            es_at = []

            def routing(n):
                if n == 0:
                    members()
                    pair_weights()
                elif n == 1:
                    es_at.append(positions())
                    one_hot_tiles()
                elif n == 2:
                    one_hot_rows(0, PAIRS)
                    expert_map(es_at[0])
                elif n == 3:
                    slot_indices()
                    weight_payload()
                elif n == 5:
                    slot_weights()

            def iteration(n, slot, turn):
                aT_lo(n)
                if is_step(n + 3):
                    xT_lo(n + 3, slot)
                if is_step(n + 2):
                    product(n + 2, (slot + 2) % R)
                if not routed(n):
                    add_shared(n)
                if isinstance(n, int) and n < FRONT:
                    routing(n)

            logits_less_max()
            for n in range(3):
                xT_lo(n, n)
            dve.wait_ge(iotas, 2)
            softmax()
            pick(0, top1)
            product(0, 0)
            take_top_out()
            pick(1, top2)
            product(1, 1)
            walk(dve, iteration)
            for t in range(TILES):
                add_choices(t)

        @block.tensor
        def _(pe):
            def three_pass(out_ap, s_hi, s_lo, m_hi, m_lo, first, last):
                pe.matmul(out_ap, s_hi, m_hi, start=first, stop=False)
                pe.matmul(out_ap, s_hi, m_lo, start=False, stop=False)
                return pe.matmul(out_ap, s_lo, m_hi, start=False, stop=last)

            pe.wait_ge(small_in, 16)
            for k in range(KC):
                ins = pe.matmul(style_ps[:, k, :], affT[:, k * P:(k + 1) * P], condT, start=True, stop=True)
            ins.then_inc(style_mm, 1)
            pe.wait_ge(wsq_done, 1)
            pe.wait_ge(consts, 2)
            wsq = base[:, 0:4, :].rearrange("p (k b) o -> p k b o", k=KC)
            for oc in range(KC):
                for b in range(batches):
                    for k in range(KC):
                        ins = pe.matmul(dem_ps[:, oc, b:b + 1], wsq[:, k, b, oc * P:(oc + 1) * P], ones[:, 0:1],
                                        start=(k == 0), stop=(k == KC - 1))
            ins.then_inc(dem_mm, 1)

            def cond(n, slot, lap):
                pe.wait_ge(x_lo_done, n + 1)
                if not isinstance(n, int) or n >= 2:
                    pe.wait_ge(y_scaled, n - 1)
                tiles_per_batch = TILES // batches
                bb = n // tiles_per_batch if isinstance(n, int) else lap // (tiles_per_batch // RING)
                for k in range(KC):
                    ins = three_pass(cond_ps[slot % 2].rearrange("p (o c) -> p o c", o=1), x_split[:, 0, slot, k, :], x_split[:, 1, slot, k, :],
                                     ws_hi[:, k, bass.ds(bb, 1), :], ws_lo[:, k, bass.ds(bb, 1), :], k == 0, k == KC - 1)
                ins.then_inc(cond_mm, 1)

            def transpose_y(n, slot):
                pe.wait_ge(y_done, n + 1)
                if not isinstance(n, int) or n >= 2:
                    pe.wait_ge(yT_lo_done, n - 1)
                for k in range(KC):
                    ins = pe.transpose(yT_ps[slot % 2][:, k, :], y_row[:, slot, k * P:(k + 1) * P], ident[:, :])
                ins.then_inc(yT_mm, 1)

            def logits(n, slot):
                pe.wait_ge(yT_lo_done, n + 1)
                for k in range(KC):
                    ins = three_pass(logit_ps[:, bass.ds(n, 1), :], yT[:, 0, slot, k, :], yT[:, 1, slot, k, :],
                                     gate_s[:, 0, k, :].unsqueeze(1), gate_s[:, 1, k, :].unsqueeze(1), k == 0, k == KC - 1)
                ins.then_inc(logit_mm, 1)

            def tile_step(n, slot, lap):
                cond(n, slot, lap)
                m, s = lag(n, slot, 2)
                if m is not None:
                    transpose_y(m, s)
                m, s = lag(n, slot, 4)
                if m is not None:
                    logits(m, s)

            pe.wait_ge(ws_split, 4)
            cond(0, 0, 0)
            cond(1, 1, 0)
            pe.wait_ge(diag_done, 1)
            for b in range(batches):
                for oc in range(KC):
                    ins = pe.matmul(demod_ps[:, b, oc * P:(oc + 1) * P], ones[:, :], diag[:, oc, b, :],
                                    start=True, stop=True)
            ins.then_inc(demod_mm, 1)
            cond(2, 2, 0)
            transpose_y(0, 0)
            cond(3, 3, 0)
            transpose_y(1, 1)
            with pe.Fori(1, TILES // RING) as lap:
                for j in range(RING):
                    tile_step(lap * RING + j, j, lap)
            logits(TILES - 4, 0)
            transpose_y(TILES - 2, RING - 2)
            logits(TILES - 3, 1)
            transpose_y(TILES - 1, RING - 1)
            logits(TILES - 2, 2)
            logits(TILES - 1, 3)

            def t1(n, slot, turn):
                if routed(n):
                    pe.wait_ge(gathered[slot], (turn - FRONT // R + 1) * 16)
                else:
                    pe.wait_ge(rows_in[slot], 16 * (shared_tile(n) // R + 1))
                if not isinstance(n, int) or n >= 1:
                    pe.wait_ge(xT_lo_done, n)
                for k in range(KC):
                    ins = pe.transpose(t1_ps[:, k, :], x_in_sb[:, slot, k * P:(k + 1) * P], ident[:, :])
                ins.then_inc(t1_mm, 1)

            def expert(n):
                if not routed(n):
                    return 0
                return pe.value_load(emap[0:1, bass.ds(slot_tile(n), 1)], min_val=1, max_val=E)

            def gate_up(n, slot):
                f = expert(n)
                pe.wait_ge(xT_lo_done, n + 1)
                if not isinstance(n, int) or n >= R:
                    pe.wait_ge(product_done, n - R + 1)
                for k in range(KC):
                    ins = three_pass(gu[slot][:, :].unsqueeze(1), xT_s[slot][:, 0, k, :], xT_s[slot][:, 1, k, :],
                                     w_hi[:, bass.ds(f, 1), k, 0:2 * F], w_lo[:, bass.ds(f, 1), k, 0:2 * F],
                                     k == 0, k == KC - 1)
                ins.then_inc(gu_mm, 1)

            def t2(n, slot):
                pe.wait_ge(product_done, n + 1)
                if not isinstance(n, int) or n >= 1:
                    pe.wait_ge(aT_lo_done, n)
                for k in range(KC):
                    ins = pe.transpose(t2_ps[:, k, :], hidden[:, 1, slot, k * P:(k + 1) * P], ident[:, :])
                ins.then_inc(t2_mm, 1)

            def down(n):
                f = expert(n)
                pe.wait_ge(aT_lo_done, n + 1)
                if not isinstance(n, int) or n >= 1:
                    pe.wait_ge(z_read, n)
                for k in range(KC):
                    ins = three_pass(z_ps[:, :].unsqueeze(1), aT[:, 0, k, :], aT[:, 1, k, :],
                                     w_hi[:, bass.ds(f, 1), k, 2 * F:FFN_W], w_lo[:, bass.ds(f, 1), k, 2 * F:FFN_W],
                                     k == 0, k == KC - 1)
                ins.then_inc(down_mm, 1)

            def prefixes():
                pe.wait_ge(member_done, 1)
                pe.matmul(before_ps[:, :, :], below[:, :], member[:, :, :], start=True, stop=True)
                pe.matmul(total_ps[:, :, :], ones_b[:, :], member[:, :, :], start=True, stop=True).then_inc(before_mm, 1)

            def invert(out_ap, pieces, done):
                for q in range(PAIRS):
                    ins = pe.matmul(out_ap, one_lo[:, q, :], pay[:, 0:pieces, q, :],
                                    start=(q == 0), stop=(q == PAIRS - 1))
                ins.then_inc(done, 1)

            def routing(n):
                if n == 0:
                    prefixes()
                elif n == 2:
                    pe.wait_ge(one_lo_done, 1)
                    pe.wait_ge(id_pay_done, 2)
                    invert(slot_id_ps, 2, id_mm)
                elif n == 4:
                    pe.wait_ge(w_pay_done, 3)
                    invert(slot_w_ps, 3, w_mm)
                elif n == 5:
                    pe.wait_ge(emap_done, 1)
                    pe.wait_ge(w_lo_done, NF)

            def iteration(n, slot, turn):
                t2(n, slot)
                if is_step(n + 3):
                    t1(n + 3, slot, turn + 1)
                if is_step(n + 2):
                    gate_up(n + 2, (slot + 2) % R)
                down(n)
                if isinstance(n, int) and n < FRONT:
                    routing(n)

            pe.wait_ge(w_lo_done, 1)
            for n in range(3):
                t1(n, n, 0)
            gate_up(0, 0)
            gate_up(1, 1)
            walk(pe, iteration)


_OUT = "out_dram"


def kernel(**inputs):
    import numpy as np
    import concourse.bacc as bacc
    from concourse.bass_utils import run_bass_kernel_spmd

    a = {k: np.asarray(v) for k, v in inputs.items()}
    x = a["x"]
    B, L, C = x.shape
    E = a["L0_ffn_gate_w"].shape[1]
    chunks = lambda m: m.reshape(C // P, P, -1).transpose(1, 0, 2).reshape(P, -1)
    small = np.concatenate([a["L0_cond_affine_w"].T, a["cond_512"].T, chunks(a["L0_cond_affine_b"]),
                            chunks(a["L0_cond_weight"].T), chunks(a["L0_ffn_gate_w"])], axis=1)
    both = lambda n: np.concatenate([a["L0_ffn_sw_" + n][None], a["L0_ffn_ew_" + n]], axis=0)
    ffn = np.concatenate([both("gate"), both("up"), both("down")], axis=2)
    ffn = ffn.reshape(E + 1, C // P, P, ffn.shape[2]).transpose(0, 2, 1, 3)
    arrays = {"xT": x.reshape(B * L // P, P, C // P, P).transpose(0, 3, 2, 1), "x_rows": x.reshape(B * L, C),
              "small": small, "bias": a["L0_cond_bias"], "ffn_w": ffn}
    arrays = {n: np.ascontiguousarray(v) for n, v in arrays.items()}

    nc = bacc.Bacc("TRN2", target_bir_lowering=False, num_devices=1)
    aps = {n: nc.dram_tensor(n, v.shape, mybir.dt.from_np(v.dtype), kind="ExternalInput").ap()
           for n, v in arrays.items()}
    out = nc.dram_tensor(_OUT, (B * L, C), F32, kind="ExternalOutput").ap()
    adaln_moe_ffn(nc, out=out, batches=B, n_experts=E, **aps)
    r = run_bass_kernel_spmd(nc, [arrays], core_ids=[0])
    return r.results[0][_OUT].reshape(B, L, C)
```

```python
from contextlib import ExitStack

import concourse.bass as bass
from concourse import mybir

P = 128
F32 = mybir.dt.float32
F32R = mybir.dt.float32r
BF16 = mybir.dt.bfloat16
I32 = mybir.dt.int32
U32 = mybir.dt.uint32
ALU = mybir.AluOpType
ACT = mybir.ActivationFunctionType
AX_X = mybir.AxisListType.X

CLAMP = 256.0
STYLE_DIM = 128
GAIN = float(STYLE_DIM) ** -0.5
DEMOD_EPS = 1e-8
TOPW_EPS = 1e-20
TOP = 2
OUT_OF_RANGE = float(1 << 20)
FAR_BELOW = -3e38


def adaln_moe_ffn(nc, xT, x_rows, small, bias, ffn_w, out, batches, n_experts):
    T, C = x_rows.shape
    KC = C // P
    F = C
    FFN_W = 2 * F + C
    E = n_experts
    NF = E + 1
    TILES = T // P
    RING = 4
    PAIRS = TOP * TILES
    ROUTED = PAIRS + E - 1
    SLOTS = ROUTED + 1
    TURNS = ROUTED // 3
    MAPPED = ROUTED + 3
    FRONT = 12
    STEPS = TILES + ROUTED
    R = 3
    INVERT = 4
    LOOP = (FRONT + R, FRONT + ROUTED - R)
    assert FRONT % R == 0 and ROUTED % R == 0 and KC == 2 and TILES % RING == 0

    at, col = 0, {}
    for name, n in (("affT", C), ("condT", batches), ("affb", KC), ("WT", KC * C), ("gate", KC * E)):
        col[name] = slice(at, at + n)
        at += n
    SMALL = at

    y_rows = nc.dram_tensor("y_rows", (T, C), F32).ap()
    z_rows = nc.dram_tensor("z_rows", (TOP * T, C), F32).ap()

    with ExitStack() as ctx:
        def sb(name, shape, dt=F32):
            return ctx.enter_context(nc.sbuf_tensor(name, shape, dt))

        def psum(name, shape, dt=F32):
            return ctx.enter_context(nc.psum_tensor(name, shape, dt))

        def sem(name):
            return ctx.enter_context(nc.semaphore(name))

        def sems(name, n):
            return [sem(f"{name}{i}") for i in range(n)]

        w_hi = sb("w_hi", [P, NF, KC, FFN_W], F32R)
        w_lo = sb("w_lo", [P, NF, KC, FFN_W], F32R)
        w_raw = sb("w_raw", [P, 2, KC, FFN_W])
        base = sb("base", [P, TILES, C])
        x_in_sb = sb("x_in_sb", [P, R, C])
        y_row = sb("y_row", [P, RING, C])
        z_sb = y_row[:, 0:R, :]
        ident = sb("ident", [P, P])
        ones = sb("ones", [P, P])
        ZR = 6
        z_in = w_raw[:, :, :, :].rearrange("p a k n -> p (a k n)")[:, 0:ZR * TOP * C].rearrange(
            "p (n c m) -> p n c m", n=ZR, c=TOP)
        rank = sb("rank", [P, TILES, E])
        below = sb("below", [P, P], BF16)
        ones_b = sb("ones_b", [P, P], BF16)
        PADT = TILES // 2
        scan = sb("scan", [P, 2, PADT + TILES, E])
        escan = sb("escan", [P, 3, E // 2 + E])
        iota_row = sb("iota_row", [P, P], BF16)
        iota_slot = sb("iota_slot", [P, SLOTS, PAIRS], BF16)
        iota_map = sb("iota_map", [P, MAPPED])
        iota_pair = sb("iota_pair", [P, PAIRS], BF16)
        part = sb("part", [P, 1])
        slot_g = sb("slot_g", [P, SLOTS], U32)
        slot_s = sb("slot_s", [P, SLOTS], U32)
        slot_w = sb("slot_w", [P, SLOTS])
        packs = sb("packs", [P, 2, TURNS])
        packs_i = sb("packs_i", [P, TURNS], I32)

        with ExitStack() as stage1:
            ws1 = lambda name, shape, dt=F32: stage1.enter_context(nc.sbuf_tensor(name, shape, dt))
            small_sb = ws1("small_sb", [P, SMALL])
            bias_bc = ws1("bias_bc", [P, C])
            demod_bc = ws1("demod_bc", [P, batches, C])
            dem = ws1("dem", [P, 3, batches, C])
            ws = ws1("ws", [P, KC, batches, C])
            wsq = ws1("wsq", [P, KC, batches, C])
            ws_hi = ws1("ws_hi", [P, KC, batches, C], F32R)
            ws_lo = ws1("ws_lo", [P, KC, batches, C], F32R)
            gate_s = ws1("gate_s", [P, 2, KC, E], F32R)
            styles = ws1("styles", [P, KC, batches])
            x_raw = ws1("x_raw", [P, RING, KC, P])
            x_split = ws1("x_split", [P, 2, RING, KC, P], F32R)
            yT = ws1("yT", [P, 2, RING, KC, P], F32R)

        xT_s = sb("xT_s", [P, R, 2, KC, P], F32R)
        aT = sb("aT", [P, 2, KC, P], F32R)
        hidden = sb("hidden", [P, 2, R, F])
        less = sb("less", [P, TILES, E])
        prob = sb("prob", [P, TILES, E])
        tmp = sb("tmp", [P, TILES, E])
        hit = sb("hit", [P, TOP, TILES, E])
        posh = sb("posh", [P, TOP, TILES, E])
        stat = sb("stat", [P, 8, TILES])
        member = sb("member", [P, TILES, E], BF16)
        tiles_i = sb("tiles_i", [P, E], I32)
        pos = sb("pos", [P, PAIRS])
        pos_i = sb("pos_i", [P, 3, PAIRS], I32)
        pos_lo = sb("pos_lo", [P, PAIRS])
        pos_hi = sb("pos_hi", [P, PAIRS], BF16)
        one_lo = sb("one_lo", [P, PAIRS, P], BF16)
        one_hi = sb("one_hi", [P, SLOTS, PAIRS], BF16)
        pay = sb("pay", [P, 5, SLOTS, PAIRS], BF16)
        w_pair = sb("w_pair", [P, 3, PAIRS])
        w_bits = sb("w_bits", [P, 3, PAIRS], BF16)
        slot_f = sb("slot_f", [P, 4, SLOTS])
        emap_c = sb("emap_c", [P, MAPPED, E])
        emap_f = sb("emap_f", [P, MAPPED])

        gu = [psum(f"gu{i}", [P, 2 * F]) for i in range(R)]
        t1_ps = psum("t1_ps", [P, KC, P])
        t2_ps = psum("t2_ps", [P, KC, P])
        z_ps = psum("z_ps", [P, C])
        logit_bank = psum("logit_bank", [P, 512])
        logit_ps = logit_bank[:, 0:TILES * E].rearrange("p (t e) -> p t e", t=TILES)
        misc_ps = psum("misc_ps", [P, 512])
        style_ps = misc_ps[:, 0:KC * batches].rearrange("p (k b) -> p k b", k=KC)
        before_ps = misc_ps[:, 0:TILES * E].rearrange("p (t e) -> p t e", t=TILES)
        total_ps = misc_ps[:, TILES * E:2 * TILES * E].rearrange("p (t e) -> p t e", t=TILES)
        slot_ps = misc_ps[:, 2 * TILES * E:2 * TILES * E + 5 * SLOTS].rearrange("p (a s) -> p a s", a=5)
        cond_ps = [gu[0][:, 0:C], gu[1][:, 0:C]]
        yT_ps = [t1_ps, t2_ps]
        demod_ps = gu[2][:, :].rearrange("p (b o) -> p b o", b=batches)

        small_in = sem("small_in")
        bias_in = sem("bias_in")
        xT_in = sems("xT_in", RING)
        w_in = sems("w_in", 2)
        base_in = sems("base_in", 2)
        consts = sem("consts")
        iotas = sem("iotas")
        style_mm = sem("style_mm")
        dve_prep = sem("dve_prep")
        wsq_done = sem("wsq_done")
        demod_mm = sem("demod_mm")
        demod_sqrt = sem("demod_sqrt")
        ws_split = sem("ws_split")
        x_hi_done = sem("x_hi_done")
        x_lo_done = sem("x_lo_done")
        cond_mm = sem("cond_mm")
        y_scaled = sem("y_scaled")
        y_biased = sem("y_biased")
        y_done = sem("y_done")
        y_stored = sems("y_stored", RING)
        yT_mm = sem("yT_mm")
        yT_hi_done = sem("yT_hi_done")
        yT_lo_done = sem("yT_lo_done")
        logit_mm = sem("logit_mm")
        w_hi_done = sem("w_hi_done")
        w_lo_done = sem("w_lo_done")
        rt = sem("rt")
        exp_ready = sem("exp_ready")
        exp_done = sem("exp_done")
        member_done = sem("member_done")
        before_mm = sem("before_mm")
        one_lo_done = sem("one_lo_done")
        pay_done = sem("pay_done")
        slots_mm = sem("slots_mm")
        slots_done = sem("slots_done")
        emap_done = sem("emap_done")
        rows_in = sems("rows_in", R)
        gathered = sems("gathered", R)
        t1_mm = sem("t1_mm")
        xT_hi_done = sem("xT_hi_done")
        xT_lo_done = sem("xT_lo_done")
        gu_mm = sem("gu_mm")
        silu_done = sem("silu_done")
        product_done = sem("product_done")
        t2_mm = sem("t2_mm")
        aT_hi_done = sem("aT_hi_done")
        aT_lo_done = sem("aT_lo_done")
        down_mm = sem("down_mm")
        z_read = sem("z_read")
        z_out = sems("z_out", R)
        z_back = sems("z_back", ZR)
        fin1 = sem("fin1")
        fin2 = sem("fin2")
        stored = sem("stored")

        f32 = lambda ap: ap.bitcast(F32)
        affT, condT, affb = (small_sb[:, col[n]] for n in ("affT", "condT", "affb"))
        WT = small_sb[:, col["WT"]].rearrange("p (k o) -> p k o", k=KC)
        gate_w = small_sb[:, col["gate"]].rearrange("p (k e) -> p k e", k=KC)
        x_rows_v = x_rows.rearrange("(n p) c -> p n c", p=P)
        out_v = out.rearrange("(n p) c -> p n c", p=P)
        y_v = y_rows.rearrange("(n p) c -> p n c", p=P)
        z_v = z_rows.rearrange("(a n p) c -> p n a c", p=P, a=TOP)

        def routed(n):
            return not isinstance(n, int) or FRONT <= n < FRONT + ROUTED

        def shared_tile(n):
            return n if n < FRONT else n - ROUTED

        def slot_tile(n):
            return n - FRONT

        def walk(eng, iteration, start=0):
            for n in range(start, LOOP[0]):
                iteration(n, n % R, n // R)
            with eng.Fori(LOOP[0] // R, LOOP[1] // R) as turn:
                for j in range(R):
                    iteration(turn * R + j, j, turn)
            for n in range(LOOP[1], STEPS):
                iteration(n, n % R, n // R)

        def is_step(n):
            return not isinstance(n, int) or n < STEPS

        def walk_tiles(eng, tile_step):
            for n in range(RING):
                tile_step(n, n, 0)
            with eng.Fori(1, TILES // RING) as lap:
                for j in range(RING):
                    tile_step(lap * RING + j, j, lap)

        def lag(n, slot, by):
            if isinstance(n, int) and n < by:
                return None, None
            return n - by, (slot - by) % RING

        block = ctx.enter_context(nc.Block())

        @block.sync
        def _(sp):
            def load_x(n):
                if n >= RING:
                    sp.wait_ge(x_hi_done, n - RING + 1)
                    sp.wait_ge(x_lo_done, n - RING + 1)
                sp.dma_start(x_raw[:, n % RING, :, :], xT[n]).then_inc(xT_in[n % RING], 16)

            def store_y(n):
                sp.wait_ge(y_done, n + 1)
                sp.dma_start(y_v[:, n, :], y_row[:, n % RING, :]).then_inc(y_stored[n % RING], 16)

            def load_rows(n):
                if n >= R:
                    sp.wait_ge(t1_mm, n - R + 1)
                t = shared_tile(n)
                sp.wait_ge(y_stored[t % RING], 16 * (t // RING + 1))
                sp.dma_start(x_in_sb[:, n % R, :], y_v[:, t, :]).then_inc(rows_in[n % R], 16)

            sp.dma_start(small_sb[:, :], small).then_inc(small_in, 16)
            for n in range(RING):
                load_x(n)
            sp.dma_start(bias_bc[:, :], bias.rearrange("(o c) -> o c", o=1).broadcast_to([P, C])).then_inc(bias_in, 16)
            for n in range(RING, TILES):
                load_x(n)
                store_y(n - RING)
                if n in (8, 12):
                    h = (n - 8) // 4 * (TILES // 2)
                    sp.dma_start(base[:, h:h + TILES // 2, :], x_rows_v[:, h:h + TILES // 2, :]).then_inc(base_in[h * 2 // TILES], 16)
            for n in range(R):
                load_rows(n)
            for n in range(TILES - RING, TILES):
                store_y(n)
            for n in range(R, FRONT):
                load_rows(n)
            for n in range(FRONT + ROUTED, STEPS):
                load_rows(n)
            for slot in range(R):
                sp.wait_ge(z_out[slot], 16 * (ROUTED // R))

            def load_z(t):
                if t >= ZR:
                    sp.wait_ge(fin2, t - ZR + 1)
                sp.dma_start(z_in[:, t % ZR, :, :], z_v[:, t, :, :]).then_inc(z_back[t % ZR], 16)

            def store(t):
                sp.wait_ge(fin2, t + 1)
                sp.dma_start(out_v[:, t, :], base[:, t, :]).then_inc(stored, 16)

            for t in range(ZR):
                load_z(t)
            for t in range(TILES):
                store(t)
                if t + ZR < TILES:
                    load_z(t + ZR)
            sp.wait_ge(stored, 16 * TILES)

        @block.gpsimd
        def _(pool):
            pool.memset(ones[:, :], 1.0)
            pool.memset(ident[:, :], 0.0).then_inc(consts, 1)
            pool.wait_ge(consts, 1)
            pool.affine_select(out=ident[:, :], in_=ident[:, :], compare_op=ALU.not_equal, fill=1.0,
                               base=0, pattern=[[-1, P]], channel_multiplier=1).then_inc(consts, 1)
            def split_w(f):
                pool.wait_ge(w_in[f % 2], 16 * (f // 2 + 1))
                pool.wait_ge(w_hi_done, f + 1)
                pool.tensor_tensor(w_lo[:, f, :, :], w_raw[:, f % 2, :, :], f32(w_hi[:, f, :, :]),
                                   ALU.subtract).then_inc(w_lo_done, 1)

            def x_lo(n):
                pool.wait_ge(xT_in[n % RING], 16 * (n // RING + 1))
                pool.wait_ge(x_hi_done, n + 1)
                pool.tensor_tensor(x_split[:, 1, n % RING, :, :], x_raw[:, n % RING, :, :],
                                   f32(x_split[:, 0, n % RING, :, :]), ALU.subtract).then_inc(x_lo_done, 1)

            for n in range(TILES):
                x_lo(n)
                if n == 3:
                    for e in range(E):
                        pool.memset(rank[:, :, e:e + 1], float(E - e))
                    pool.memset(ones_b[:, :], 1.0)
                    pool.memset(scan[:, :, :, :], 0.0)
                    pool.memset(escan[:, :, :], 0.0).then_inc(iotas, 1)
                    pool.iota(iota_row[:, :], [[1, P]], base=0, channel_multiplier=0,
                              allow_small_or_imprecise_dtypes=True)
                    pool.iota(iota_slot[:, :, :], [[1, SLOTS], [0, PAIRS]], base=0, channel_multiplier=0,
                              allow_small_or_imprecise_dtypes=True)
                    pool.iota(iota_map[:, :], [[1, MAPPED]], base=0, channel_multiplier=0,
                              allow_small_or_imprecise_dtypes=True)
                    pool.iota(iota_pair[:, :], [[1, PAIRS]], base=1, channel_multiplier=0,
                              allow_small_or_imprecise_dtypes=True)
                    pool.iota(part[:, :], [[0, 1]], base=0, channel_multiplier=1,
                              allow_small_or_imprecise_dtypes=True)
                    pool.wait_ge(iotas, 1)
                    pool.affine_select(out=below[:, :], in_=ones_b[:, :], compare_op=ALU.is_gt, fill=0.0,
                                       base=0, pattern=[[1, P]], channel_multiplier=-1).then_inc(iotas, 1)
                if n in (4, 8, 12):
                    split_w(n // 4 - 1)
            for f in range(3, NF):
                split_w(f)

            def gather(n):
                pool.wait_ge(t1_mm, n - R + 1)
                r = slot_tile(n)
                pool.indirect_dma_start(x_in_sb[:, n % R, :], None, y_rows,
                                        bass.IndirectOffsetOnAxis(ap=slot_g[:, r:r + 1], axis=0)
                                        ).then_inc(gathered[n % R], 16)

            def scatter(n):
                pool.wait_ge(z_read, n + 1)
                r = slot_tile(n)
                pool.indirect_dma_start(z_rows, bass.IndirectOffsetOnAxis(ap=slot_s[:, r:r + 1], axis=0),
                                        z_sb[:, n % R, :], None, bounds_check=TOP * T - 1,
                                        oob_is_err=False).then_inc(z_out[n % R], 16)

            pool.wait_ge(slots_done, 1)
            for slot in range(RING):
                pool.wait_ge(y_stored[slot], 16 * (TILES // RING))
            for n in range(FRONT, FRONT + 2 * R):
                gather(n)
            for n in range(FRONT, FRONT + ROUTED):
                if n + 2 * R < FRONT + ROUTED:
                    gather(n + 2 * R)
                scatter(n)

        @block.scalar
        def _(act):
            def load_w(f):
                if f >= 2:
                    act.wait_ge(w_hi_done, f - 1)
                    act.wait_ge(w_lo_done, f - 1)
                act.dma_start(w_raw[:, f % 2, :, :], ffn_w[f]).then_inc(w_in[f % 2], 16)

            def split_w(f):
                act.wait_ge(w_in[f % 2], 16 * (f // 2 + 1))
                act.copy(w_hi[:, f, :, :], w_raw[:, f % 2, :, :]).then_inc(w_hi_done, 1)
                if 2 <= f + 1 < NF:
                    load_w(f + 1)

            def x_hi(n):
                act.wait_ge(xT_in[n % RING], 16 * (n // RING + 1))
                if n >= RING:
                    act.wait_ge(cond_mm, n - RING + 1)
                act.copy(x_split[:, 0, n % RING, :, :], x_raw[:, n % RING, :, :]).then_inc(x_hi_done, 1)

            def yT_hi(n):
                act.wait_ge(yT_mm, n + 1)
                if n >= RING:
                    act.wait_ge(logit_mm, n - RING + 1)
                act.copy(yT[:, 0, n % RING, :, :], yT_ps[n % 2][:, :, :]).then_inc(yT_hi_done, 1)

            for n in range(RING):
                x_hi(n)
            load_w(0)
            load_w(1)
            act.wait_ge(dve_prep, 1 + KC * batches)
            act.activation(wsq[:, :, :, :], ws[:, :, :, :], ACT.Square).then_inc(wsq_done, 1)
            act.wait_ge(dve_prep, 2 + KC * batches)
            act.activation(dem[:, 1, :, :], dem[:, 0, :, :], ACT.Sqrt).then_inc(demod_sqrt, 1)
            for n in range(TILES):
                if n + RING < TILES:
                    x_hi(n + RING)
                yT_hi(n)
                if n in (0, 4, 8, 12):
                    split_w(n // 4)
            act.wait_ge(exp_ready, 1)
            act.activation(prob[:, :, :], less[:, :, :], ACT.Exp).then_inc(exp_done, 1)

            def xT_hi(n, slot):
                act.wait_ge(t1_mm, n + 1)
                if not isinstance(n, int) or n >= R:
                    act.wait_ge(gu_mm, n - R + 1)
                act.copy(xT_s[:, slot, 0, :, :], t1_ps[:, :, :]).then_inc(xT_hi_done, 1)

            def silu(n, slot):
                act.wait_ge(gu_mm, n + 1)
                if not isinstance(n, int) or n >= R:
                    act.wait_ge(product_done, n - R + 1)
                act.activation(hidden[:, 0, slot, :], gu[slot][:, 0:F], ACT.Silu).then_inc(silu_done, 1)

            def aT_hi(n):
                act.wait_ge(t2_mm, n + 1)
                act.copy(aT[:, 0, :, :], t2_ps[:, :, :]).then_inc(aT_hi_done, 1)

            def read_z(n, slot, turn):
                act.wait_ge(down_mm, n + 1)
                if not isinstance(n, int) or n >= FRONT + R:
                    act.wait_ge(z_out[slot], (turn - FRONT // R) * 16)
                act.copy(z_sb[:, slot, :], z_ps[:, :]).then_inc(z_read, 1)

            def iteration(n, slot, turn):
                aT_hi(n)
                if is_step(n + 3):
                    xT_hi(n + 3, slot)
                if is_step(n + 2):
                    silu(n + 2, (slot + 2) % R)
                if routed(n):
                    read_z(n, slot, turn)
                if isinstance(n, int) and n + 4 < NF:
                    split_w(n + 4)

            for n in range(3):
                xT_hi(n, n)
            silu(0, 0)
            silu(1, 1)
            walk(act, iteration)

        @block.vector
        def _(dve):
            dve.wait_ge(small_in, 16)
            dve.wait_ge(style_mm, 1)
            for k in range(KC):
                ins = dve.tensor_scalar(styles[:, k, :], style_ps[:, k, :], GAIN, affb[:, k:k + 1],
                                        ALU.mult, ALU.add)
            ins.then_inc(dve_prep, 1)
            dve.wait_ge(dve_prep, 1)
            for k in range(KC):
                for b in range(batches):
                    dve.tensor_scalar(ws[:, k, b, :], WT[:, k, :], styles[:, k, b:b + 1], None,
                                      ALU.mult).then_inc(dve_prep, 1)
            dve.tensor_copy(gate_s[:, 0, :, :], gate_w).then_inc(ws_split, 1)
            dve.wait_ge(dve_prep, 1 + KC * batches)
            dve.tensor_copy(ws_hi[:, :, :, :], ws[:, :, :, :]).then_inc(ws_split, 1)
            dve.wait_ge(ws_split, 2)
            dve.tensor_tensor(ws_lo[:, :, :, :], ws[:, :, :, :], f32(ws_hi[:, :, :, :]),
                              ALU.subtract).then_inc(ws_split, 1)
            dve.tensor_tensor(gate_s[:, 1, :, :], gate_w, f32(gate_s[:, 0, :, :]),
                              ALU.subtract).then_inc(ws_split, 1)
            v, root, c = (dem[:, i, :, :] for i in range(3))
            r = demod_bc[:, :, :]
            step = 2 + KC * batches
            dve.wait_ge(demod_mm, 1)
            dve.tensor_scalar(v, demod_ps[:, :, :], DEMOD_EPS, None, ALU.add).then_inc(dve_prep, 1)
            dve.wait_ge(demod_sqrt, 1)
            dve.reciprocal(r, root).then_inc(dve_prep, 1)
            dve.wait_ge(dve_prep, step + 1)
            dve.tensor_tensor(c, r, r, ALU.mult).then_inc(dve_prep, 1)
            dve.wait_ge(dve_prep, step + 2)
            dve.scalar_tensor_tensor(out=c, in0=c, scalar=-0.5, in1=v, op0=ALU.mult, op1=ALU.mult).then_inc(dve_prep, 1)
            dve.wait_ge(dve_prep, step + 3)
            dve.scalar_tensor_tensor(out=r, in0=c, scalar=1.5, in1=r, op0=ALU.add, op1=ALU.mult).then_inc(dve_prep, 1)
            dve.wait_ge(dve_prep, step + 4)

            def scale_y(n, slot, lap):
                first = isinstance(n, int) and n < RING
                dve.wait_ge(cond_mm, n + 1)
                if not first:
                    dve.wait_ge(y_stored[slot], lap * 16)
                    dve.wait_ge(yT_mm, n - RING + 1)
                tiles_per_batch = TILES // batches
                bb = n // tiles_per_batch if isinstance(n, int) else lap // (tiles_per_batch // RING)
                dve.tensor_tensor(y_row[:, slot, :].rearrange("p (o c) -> p o c", o=1), cond_ps[slot % 2].rearrange("p (o c) -> p o c", o=1),
                                  demod_bc[:, bass.ds(bb, 1), :], ALU.mult).then_inc(y_scaled, 1)

            def bias_y(n, slot):
                dve.wait_ge(y_scaled, n + 1)
                dve.tensor_tensor(y_row[:, slot, :], y_row[:, slot, :], bias_bc[:, :], ALU.add).then_inc(y_biased, 1)

            def clip_y(n, slot):
                dve.wait_ge(y_biased, n + 1)
                dve.tensor_scalar(y_row[:, slot, :], y_row[:, slot, :], CLAMP, -CLAMP,
                                  ALU.min, ALU.max).then_inc(y_done, 1)

            def yT_lo(n, slot):
                dve.wait_ge(yT_hi_done, n + 1)
                dve.tensor_tensor(yT[:, 1, slot, :, :], yT_ps[slot % 2][:, :, :], f32(yT[:, 0, slot, :, :]),
                                  ALU.subtract).then_inc(yT_lo_done, 1)

            def tile_step(n, slot, lap):
                scale_y(n, slot, lap)
                bias_y(n, slot)
                clip_y(n, slot)
                m, s = lag(n, slot, 3)
                if m is not None:
                    yT_lo(m, s)

            dve.wait_ge(bias_in, 16)
            walk_tiles(dve, tile_step)
            for n in range(TILES - 3, TILES):
                yT_lo(n, n % RING)

            count = [0]

            def link(ins):
                count[0] += 1
                ins.then_inc(rt, 1)
                dve.wait_ge(rt, count[0])

            bc = lambda s: s.unsqueeze(2).broadcast_to([P, TILES, E])
            mx, total, second, key, rsum = (stat[:, i, :] for i in range(5))

            def logits_less_max():
                dve.wait_ge(logit_mm, TILES)
                link(dve.tensor_reduce(mx, logit_ps[:, :, :], AX_X, ALU.max))
                dve.tensor_tensor(less[:, :, :], logit_ps[:, :, :], bc(mx), ALU.subtract).then_inc(exp_ready, 1)
                dve.wait_ge(exp_ready, 1)

            def lowest(n):
                h = hit[:, n, :, :]
                link(dve.tensor_reduce(key, h, AX_X, ALU.max))
                link(dve.tensor_tensor(h, h, bc(key), ALU.is_equal))

            def pick_first():
                link(dve.scalar_tensor_tensor(out=hit[:, 0, :, :], in0=less[:, :, :], scalar=0.0,
                                              in1=rank[:, :, :], op0=ALU.is_equal, op1=ALU.mult))
                lowest(0)

            def pick_second():
                link(dve.scalar_tensor_tensor(out=tmp[:, :, :], in0=hit[:, 0, :, :], scalar=FAR_BELOW,
                                              in1=less[:, :, :], op0=ALU.mult, op1=ALU.add))
                link(dve.tensor_reduce(second, tmp[:, :, :], AX_X, ALU.max))
                link(dve.tensor_tensor(hit[:, 1, :, :], tmp[:, :, :], bc(second), ALU.is_equal))
                link(dve.tensor_tensor(hit[:, 1, :, :], hit[:, 1, :, :], rank[:, :, :], ALU.mult))
                lowest(1)

            def members():
                dve.tensor_tensor(member[:, :, :], hit[:, 0, :, :], hit[:, 1, :, :], ALU.add).then_inc(member_done, 1)

            def pair_weights():
                dve.wait_ge(exp_done, 1)
                link(dve.tensor_reduce(total, prob[:, :, :], AX_X, ALU.add))
                link(dve.tensor_tensor(posh[:, 1, :, :], prob[:, :, :], hit[:, 1, :, :], ALU.mult))
                link(dve.tensor_tensor(posh[:, 0, :, :], prob[:, :, :], hit[:, 0, :, :], ALU.mult))
                link(dve.tensor_reduce(w_pair[:, 1, :], posh[:, :, :, :].rearrange("p a t e -> p (a t) e"), AX_X, ALU.add))
                link(dve.reciprocal(total, total))
                for a in range(TOP):
                    link(dve.tensor_tensor(w_pair[:, 1, a * TILES:(a + 1) * TILES],
                                           w_pair[:, 1, a * TILES:(a + 1) * TILES], total, ALU.mult))
                link(dve.tensor_tensor(rsum, w_pair[:, 1, 0:TILES], w_pair[:, 1, TILES:PAIRS], ALU.add))
                link(dve.tensor_scalar(rsum, rsum, TOPW_EPS, None, ALU.add))
                link(dve.reciprocal(rsum, rsum))
                for a in range(TOP):
                    link(dve.tensor_tensor(w_pair[:, 0, a * TILES:(a + 1) * TILES],
                                           w_pair[:, 1, a * TILES:(a + 1) * TILES], rsum, ALU.mult))
                for i in range(3):
                    link(dve.tensor_copy(w_bits[:, i, :], w_pair[:, i, :]))
                    if i < 2:
                        link(dve.tensor_tensor(w_pair[:, i + 1, :], w_pair[:, i, :], w_bits[:, i, :], ALU.subtract))

            def positions():
                dve.wait_ge(before_mm, 1)
                link(dve.tensor_copy(scan[:, 0, PADT:, :], total_ps[:, :, :]))
                src = 0
                for d in (1, 2, 4, 8):
                    link(dve.tensor_tensor(scan[:, 1 - src, PADT:, :], scan[:, src, PADT:, :],
                                           scan[:, src, PADT - d:PADT + TILES - d, :], ALU.add))
                    src = 1 - src
                last = scan[:, src, PADT + TILES - 1, :]
                link(dve.tensor_scalar(tiles_i[:, :], last, float(P - 1), None, ALU.add))
                link(dve.tensor_scalar(tiles_i[:, :], tiles_i[:, :], 7, None, ALU.logical_shift_right))
                H = E // 2
                link(dve.tensor_copy(escan[:, 0, H:], tiles_i[:, :]))
                es = 0
                for d in (1, 2, 4):
                    link(dve.tensor_tensor(escan[:, 1 - es, H:], escan[:, es, H:], escan[:, es, H - d:H + E - d], ALU.add))
                    es = 1 - es
                link(dve.tensor_tensor(escan[:, 2, H:], escan[:, es, H:], tiles_i[:, :], ALU.subtract))
                link(dve.tensor_scalar(escan[:, 2, H:], escan[:, 2, H:], float(P), None, ALU.mult))
                link(dve.tensor_tensor(tmp[:, :, :], scan[:, src, PADT:, :], total_ps[:, :, :], ALU.subtract))
                link(dve.tensor_tensor(tmp[:, :, :], tmp[:, :, :], before_ps[:, :, :], ALU.add))
                link(dve.tensor_tensor(tmp[:, :, :], tmp[:, :, :],
                                       escan[:, 2, H:].unsqueeze(1).broadcast_to([P, TILES, E]), ALU.add))
                for a in range(TOP):
                    link(dve.tensor_tensor(posh[:, a, :, :], hit[:, a, :, :], tmp[:, :, :], ALU.mult))
                link(dve.tensor_reduce(pos[:, :], posh[:, :, :, :].rearrange("p a t e -> p (a t) e"), AX_X, ALU.add))
                link(dve.tensor_copy(pos_i[:, 0, :], pos[:, :]))
                link(dve.tensor_scalar(pos_i[:, 1, :], pos_i[:, 0, :], P - 1, None, ALU.bitwise_and))
                link(dve.tensor_scalar(pos_i[:, 2, :], pos_i[:, 0, :], 7, None, ALU.logical_shift_right))
                link(dve.tensor_copy(pos_lo[:, :], pos_i[:, 1, :]))
                link(dve.tensor_copy(pos_hi[:, :], pos_i[:, 2, :]))
                return es

            def expert_map(es):
                H = E // 2
                link(dve.tensor_tensor(emap_c[:, :, :], iota_map[:, :].unsqueeze(2).broadcast_to([P, MAPPED, E]),
                                       escan[:, es, H:].unsqueeze(1).broadcast_to([P, MAPPED, E]), ALU.is_ge))
                link(dve.tensor_reduce(emap_f[:, :], emap_c[:, :, :], AX_X, ALU.add))
                link(dve.tensor_scalar(emap_f[:, :], emap_f[:, :], float(E - 1), 1.0, ALU.min, ALU.add))
                at_step = lambda j: emap_f[:, (j // R) * R:(j // R) * R + ROUTED].rearrange(
                    "p (t r) -> p t r", r=R)[:, :, j % R]
                link(dve.scalar_tensor_tensor(out=packs[:, 0, :], in0=at_step(4), scalar=16.0, in1=at_step(3),
                                              op0=ALU.mult, op1=ALU.add))
                link(dve.scalar_tensor_tensor(out=packs[:, 1, :], in0=packs[:, 0, :], scalar=16.0, in1=at_step(2),
                                              op0=ALU.mult, op1=ALU.add))
                link(dve.scalar_tensor_tensor(out=packs[:, 0, :], in0=packs[:, 1, :], scalar=16.0, in1=at_step(1),
                                              op0=ALU.mult, op1=ALU.add))
                dve.scalar_tensor_tensor(out=packs_i[:, :], in0=packs[:, 0, :], scalar=16.0, in1=at_step(0),
                                         op0=ALU.mult, op1=ALU.add).then_inc(emap_done, 1)

            def one_hot_rows(a, b):
                for q in range(a, b):
                    ins = dve.tensor_scalar(one_lo[:, q, :], iota_row[:, :], pos_lo[:, q:q + 1], None, ALU.is_equal)
                ins.then_inc(one_lo_done, 1)

            over_slots = lambda m: m.unsqueeze(1).broadcast_to([P, SLOTS, PAIRS])

            def one_hot_tiles():
                link(dve.tensor_tensor(one_hi[:, :, :], iota_slot[:, :, :], over_slots(pos_hi[:, :]), ALU.is_equal))
                dve.tensor_tensor(pay[:, 0, :, :], one_hi[:, :, :], over_slots(iota_pair[:, :]), ALU.mult).then_inc(pay_done, 1)
                dve.tensor_scalar(pay[:, 1, :, :], one_hi[:, :, :], part[:, 0:1], None, ALU.mult).then_inc(pay_done, 1)

            def weight_payload():
                for i in range(3):
                    dve.tensor_tensor(pay[:, 2 + i, :, :], one_hi[:, :, :], over_slots(w_bits[:, i, :]), ALU.mult).then_inc(pay_done, 1)

            def slot_indices():
                dve.wait_ge(slots_mm, 1)
                link(dve.tensor_copy(slot_f[:, 1, :], slot_ps[:, 1, :]))
                link(dve.scalar_tensor_tensor(out=slot_f[:, 0, :], in0=slot_ps[:, 0, :], scalar=float(P),
                                              in1=slot_f[:, 1, :], op0=ALU.mult, op1=ALU.add))
                link(dve.tensor_scalar(slot_f[:, 2, :], slot_f[:, 0, :], float(T + P), float(-T), ALU.is_ge, ALU.mult))
                link(dve.scalar_tensor_tensor(out=slot_f[:, 2, :], in0=slot_f[:, 0, :], scalar=float(-P),
                                              in1=slot_f[:, 2, :], op0=ALU.add, op1=ALU.add))
                link(dve.tensor_scalar(slot_g[:, :], slot_f[:, 2, :], 0.0, None, ALU.max))
                link(dve.tensor_scalar(slot_f[:, 3, :], slot_f[:, 0, :], float(P), OUT_OF_RANGE, ALU.is_lt, ALU.mult))
                link(dve.tensor_scalar(slot_f[:, 0, :], slot_f[:, 0, :], float(-P), None, ALU.add))
                link(dve.tensor_tensor(slot_s[:, :], slot_f[:, 0, :], slot_f[:, 3, :], ALU.add))
                dve.tensor_copy(slot_f[:, 1, :], slot_f[:, 0, :]).then_inc(slots_done, 1)

            def slot_weights():
                dve.wait_ge(slots_mm, 1)
                link(dve.tensor_copy(slot_w[:, :], slot_ps[:, 2, :]))
                link(dve.tensor_tensor(slot_w[:, :], slot_w[:, :], slot_ps[:, 3, :], ALU.add))
                link(dve.tensor_tensor(slot_w[:, :], slot_w[:, :], slot_ps[:, 4, :], ALU.add))

            def xT_lo(n, slot):
                dve.wait_ge(xT_hi_done, n + 1)
                dve.tensor_tensor(xT_s[:, slot, 1, :, :], t1_ps[:, :, :], f32(xT_s[:, slot, 0, :, :]),
                                  ALU.subtract).then_inc(xT_lo_done, 1)

            def product(n, slot):
                dve.wait_ge(silu_done, n + 1)
                w = slot_w[:, bass.ds(slot_tile(n), 1)] if routed(n) else ones[:, 0:1]
                dve.scalar_tensor_tensor(out=hidden[:, 1, slot, :], in0=gu[slot][:, F:2 * F], scalar=w,
                                         in1=hidden[:, 0, slot, :], op0=ALU.mult, op1=ALU.mult).then_inc(product_done, 1)

            def aT_lo(n):
                dve.wait_ge(aT_hi_done, n + 1)
                dve.tensor_tensor(aT[:, 1, :, :], t2_ps[:, :, :], f32(aT[:, 0, :, :]),
                                  ALU.subtract).then_inc(aT_lo_done, 1)

            def add_shared(n):
                t = shared_tile(n)
                dve.wait_ge(down_mm, n + 1)
                dve.wait_ge(base_in[t // (TILES // 2)], 16)
                dve.tensor_tensor(base[:, t, :], z_ps[:, :], base[:, t, :], ALU.add).then_inc(z_read, 1)

            def add_choices(t):
                dve.wait_ge(z_back[t % ZR], 16 * (t // ZR + 1))
                if t >= FRONT:
                    dve.wait_ge(z_read, FRONT + ROUTED + t - FRONT + 1)
                dve.tensor_tensor(base[:, t, :], base[:, t, :], z_in[:, t % ZR, 0, :], ALU.add).then_inc(fin1, 1)
                dve.wait_ge(fin1, t + 1)
                dve.tensor_tensor(base[:, t, :], base[:, t, :], z_in[:, t % ZR, 1, :], ALU.add).then_inc(fin2, 1)

            es_at = []

            def routing(n):
                if n == 0:
                    es_at.append(positions())
                elif n == 1:
                    one_hot_tiles()
                    one_hot_rows(0, PAIRS // 2)
                elif n == 2:
                    one_hot_rows(PAIRS // 2, PAIRS)
                elif n == 3:
                    weight_payload()
                elif n == 4:
                    slot_indices()
                elif n == 5:
                    expert_map(es_at[0])
                elif n == 6:
                    slot_weights()

            def iteration(n, slot, turn):
                aT_lo(n)
                if is_step(n + 3):
                    xT_lo(n + 3, slot)
                if is_step(n + 2):
                    product(n + 2, (slot + 2) % R)
                if not routed(n):
                    add_shared(n)
                if isinstance(n, int) and n < FRONT:
                    routing(n)

            dve.wait_ge(iotas, 2)
            logits_less_max()
            pick_first()
            for n in range(3):
                xT_lo(n, n)
            pick_second()
            members()
            product(0, 0)
            pair_weights()
            product(1, 1)
            walk(dve, iteration)
            for t in range(TILES):
                add_choices(t)

        @block.tensor
        def _(pe):
            def three_pass(out_ap, s_hi, s_lo, m_hi, m_lo, first, last):
                pe.matmul(out_ap, s_hi, m_hi, start=first, stop=False)
                pe.matmul(out_ap, s_hi, m_lo, start=False, stop=False)
                return pe.matmul(out_ap, s_lo, m_hi, start=False, stop=last)

            pe.wait_ge(small_in, 16)
            for k in range(KC):
                ins = pe.matmul(style_ps[:, k, :], affT[:, k * P:(k + 1) * P], condT, start=True, stop=True)
            ins.then_inc(style_mm, 1)
            pe.wait_ge(wsq_done, 1)
            pe.wait_ge(consts, 2)
            for k in range(KC):
                ins = pe.matmul(demod_ps[:, :, :], ones[:, :], wsq[:, k, :, :], start=(k == 0), stop=(k == KC - 1))
            ins.then_inc(demod_mm, 1)

            def cond(n, slot, lap):
                pe.wait_ge(x_lo_done, n + 1)
                if not isinstance(n, int) or n >= 2:
                    pe.wait_ge(y_scaled, n - 1)
                tiles_per_batch = TILES // batches
                bb = n // tiles_per_batch if isinstance(n, int) else lap // (tiles_per_batch // RING)
                for k in range(KC):
                    ins = three_pass(cond_ps[slot % 2].rearrange("p (o c) -> p o c", o=1), x_split[:, 0, slot, k, :], x_split[:, 1, slot, k, :],
                                     ws_hi[:, k, bass.ds(bb, 1), :], ws_lo[:, k, bass.ds(bb, 1), :], k == 0, k == KC - 1)
                ins.then_inc(cond_mm, 1)

            def transpose_y(n, slot):
                pe.wait_ge(y_done, n + 1)
                if not isinstance(n, int) or n >= 2:
                    pe.wait_ge(yT_lo_done, n - 1)
                for k in range(KC):
                    ins = pe.transpose(yT_ps[slot % 2][:, k, :], y_row[:, slot, k * P:(k + 1) * P], ident[:, :])
                ins.then_inc(yT_mm, 1)

            def logits(n, slot):
                pe.wait_ge(yT_lo_done, n + 1)
                wide = lambda h, k: gate_s[:, h, k, :].unsqueeze(1).broadcast_to([P, TILES, E])
                for k in range(KC):
                    ins = three_pass(logit_bank[:, bass.ds(n * E, TILES * E)].rearrange("p (t e) -> p t e", t=TILES),
                                     yT[:, 0, slot, k, :], yT[:, 1, slot, k, :], wide(0, k), wide(1, k),
                                     k == 0, k == KC - 1)
                ins.then_inc(logit_mm, 1)

            def tile_step(n, slot, lap):
                cond(n, slot, lap)
                m, s = lag(n, slot, 2)
                if m is not None:
                    transpose_y(m, s)
                m, s = lag(n, slot, 4)
                if m is not None:
                    logits(m, s)

            pe.wait_ge(ws_split, 4)
            cond(0, 0, 0)
            cond(1, 1, 0)
            cond(2, 2, 0)
            transpose_y(0, 0)
            cond(3, 3, 0)
            transpose_y(1, 1)
            with pe.Fori(1, TILES // RING) as lap:
                for j in range(RING):
                    tile_step(lap * RING + j, j, lap)
            logits(TILES - 4, 0)
            transpose_y(TILES - 2, RING - 2)
            logits(TILES - 3, 1)
            transpose_y(TILES - 1, RING - 1)
            logits(TILES - 2, 2)
            logits(TILES - 1, 3)

            def t1(n, slot, turn):
                if routed(n):
                    pe.wait_ge(gathered[slot], (turn - FRONT // R + 1) * 16)
                else:
                    pe.wait_ge(rows_in[slot], 16 * (shared_tile(n) // R + 1))
                if not isinstance(n, int) or n >= 1:
                    pe.wait_ge(xT_lo_done, n)
                for k in range(KC):
                    ins = pe.transpose(t1_ps[:, k, :], x_in_sb[:, slot, k * P:(k + 1) * P], ident[:, :])
                ins.then_inc(t1_mm, 1)

            pack = pe.alloc_register("expert_pack")

            def load_pack(routed_turn):
                pe.reg_load(pack, packs_i[0:1, bass.ds(routed_turn, 1)])

            def unpack():
                word = pe.snap(pack)
                return [nc.s_assert_within(pe.snap((word >> (4 * j)) & 15), 1, E,
                                          skip_runtime_bounds_check_because="expert_map() bounds them to 1..E")
                        for j in range(R + 2)]

            def gate_up(n, slot, f):
                pe.wait_ge(xT_lo_done, n + 1)
                if not isinstance(n, int) or n >= R:
                    pe.wait_ge(product_done, n - R + 1)
                for k in range(KC):
                    ins = three_pass(gu[slot][:, :].unsqueeze(1), xT_s[:, slot, 0, k, :], xT_s[:, slot, 1, k, :],
                                     w_hi[:, bass.ds(f, 1), k, 0:2 * F], w_lo[:, bass.ds(f, 1), k, 0:2 * F],
                                     k == 0, k == KC - 1)
                ins.then_inc(gu_mm, 1)

            def t2(n, slot):
                pe.wait_ge(product_done, n + 1)
                if not isinstance(n, int) or n >= 1:
                    pe.wait_ge(aT_lo_done, n)
                for k in range(KC):
                    ins = pe.transpose(t2_ps[:, k, :], hidden[:, 1, slot, k * P:(k + 1) * P], ident[:, :])
                ins.then_inc(t2_mm, 1)

            def down(n, f):
                pe.wait_ge(aT_lo_done, n + 1)
                if not isinstance(n, int) or n >= 1:
                    pe.wait_ge(z_read, n)
                for k in range(KC):
                    ins = three_pass(z_ps[:, :].unsqueeze(1), aT[:, 0, k, :], aT[:, 1, k, :],
                                     w_hi[:, bass.ds(f, 1), k, 2 * F:FFN_W], w_lo[:, bass.ds(f, 1), k, 2 * F:FFN_W],
                                     k == 0, k == KC - 1)
                ins.then_inc(down_mm, 1)

            def prefixes():
                pe.wait_ge(member_done, 1)
                pe.matmul(before_ps[:, :, :], below[:, :], member[:, :, :], start=True, stop=True)
                pe.matmul(total_ps[:, :, :], ones_b[:, :], member[:, :, :], start=True, stop=True).then_inc(before_mm, 1)

            def invert():
                pe.wait_ge(one_lo_done, 2)
                pe.wait_ge(pay_done, 5)
                for q in range(PAIRS):
                    ins = pe.matmul(slot_ps, one_lo[:, q, :], pay[:, :, :, q],
                                    start=(q == 0), stop=(q == PAIRS - 1))
                ins.then_inc(slots_mm, 1)

            def iteration(n, slot, turn, experts):
                t2(n, slot)
                if is_step(n + 3):
                    t1(n + 3, slot, turn + 1)
                if is_step(n + 2):
                    gate_up(n + 2, (slot + 2) % R, experts[slot + 2])
                if slot == 0 and routed(n) and (not isinstance(n, int) or n + R < FRONT + ROUTED):
                    load_pack(turn - FRONT // R + 1)
                down(n, experts[slot])

            def shared_turn(turn, ahead=None):
                experts = [0] * R + (ahead[0:2] if ahead else [0, 0])
                for j in range(R):
                    if turn * R + j < STEPS:
                        iteration(turn * R + j, j, turn, experts)

            pe.wait_ge(w_lo_done, 1)
            for n in range(3):
                t1(n, n, 0)
            gate_up(0, 0, 0)
            gate_up(1, 1, 0)
            routed_from, routed_to = FRONT // R, (FRONT + ROUTED) // R
            for turn in range(routed_from - 1):
                experts = [0] * (R + 2)
                for j in range(R):
                    n = turn * R + j
                    iteration(n, j, turn, experts)
                    if n == 0:
                        prefixes()
                    if n == INVERT:
                        invert()
            pe.wait_ge(emap_done, 1)
            pe.wait_ge(w_lo_done, NF)
            load_pack(0)
            experts = unpack()
            shared_turn(routed_from - 1, experts)
            for j in range(R):
                iteration(FRONT + j, j, routed_from, experts)
            with pe.Fori(routed_from + 1, routed_to - 1) as turn:
                experts = unpack()
                for j in range(R):
                    iteration(turn * R + j, j, turn, experts)
            experts = unpack()[0:R] + [0, 0]
            for j in range(R):
                iteration((routed_to - 1) * R + j, j, routed_to - 1, experts)
            for turn in range(routed_to, -(-STEPS // R)):
                shared_turn(turn)


_OUT = "out_dram"


def kernel(**inputs):
    import numpy as np
    import concourse.bacc as bacc
    from concourse.bass_utils import run_bass_kernel_spmd

    a = {k: np.asarray(v) for k, v in inputs.items()}
    x = a["x"]
    B, L, C = x.shape
    E = a["L0_ffn_gate_w"].shape[1]
    chunks = lambda m: m.reshape(C // P, P, -1).transpose(1, 0, 2).reshape(P, -1)
    small = np.concatenate([a["L0_cond_affine_w"].T, a["cond_512"].T, chunks(a["L0_cond_affine_b"]),
                            chunks(a["L0_cond_weight"].T), chunks(a["L0_ffn_gate_w"])], axis=1)
    both = lambda n: np.concatenate([a["L0_ffn_sw_" + n][None], a["L0_ffn_ew_" + n]], axis=0)
    ffn = np.concatenate([both("gate"), both("up"), both("down")], axis=2)
    ffn = ffn.reshape(E + 1, C // P, P, ffn.shape[2]).transpose(0, 2, 1, 3)
    arrays = {"xT": x.reshape(B * L // P, P, C // P, P).transpose(0, 3, 2, 1), "x_rows": x.reshape(B * L, C),
              "small": small, "bias": a["L0_cond_bias"], "ffn_w": ffn}
    arrays = {n: np.ascontiguousarray(v) for n, v in arrays.items()}

    nc = bacc.Bacc("TRN2", target_bir_lowering=False, num_devices=1)
    aps = {n: nc.dram_tensor(n, v.shape, mybir.dt.from_np(v.dtype), kind="ExternalInput").ap()
           for n, v in arrays.items()}
    out = nc.dram_tensor(_OUT, (B * L, C), F32, kind="ExternalOutput").ap()
    adaln_moe_ffn(nc, out=out, batches=B, n_experts=E, **aps)
    r = run_bass_kernel_spmd(nc, [arrays], core_ids=[0])
    return r.results[0][_OUT].reshape(B, L, C)
```

```python
from contextlib import ExitStack

import concourse.bass as bass
from concourse import mybir

P = 128
F32 = mybir.dt.float32
F32R = mybir.dt.float32r
BF16 = mybir.dt.bfloat16
I32 = mybir.dt.int32
U32 = mybir.dt.uint32
ALU = mybir.AluOpType
ACT = mybir.ActivationFunctionType
AX_X = mybir.AxisListType.X

GROUP_TOKENS = 4 * P

CLAMP = 256.0
STYLE_DIM = 128
GAIN = float(STYLE_DIM) ** -0.5
DEMOD_EPS = 1e-8
TOPW_EPS = 1e-20
TOP = 2
OUT_OF_RANGE = float(1 << 20)
FAR_BELOW = -3e38


def adaln_moe_ffn(nc, xT, x_rows, small, ffn_w, out, batches, n_experts):
    T, C = x_rows.shape
    KC = C // P
    F = C
    FFN_W = 2 * F + C
    E = n_experts
    NF = E + 1
    TILES = T // P
    WIDE = 12
    GT = GROUP_TOKENS // P
    GROUPS = TILES // GT
    PAIRS = TOP * TILES
    ROUTED = PAIRS + E - 1
    SLOTS = ROUTED + 1
    TURNS = ROUTED // 3
    MAPPED = ROUTED + 3
    FRONT = 6
    BEHIND = FRONT + ROUTED
    STEPS = TILES + ROUTED
    ADDS_FROM = BEHIND + 2
    R = 3
    INVERT = 1
    WB = 3
    ZR = 9
    POOL_SPLITS, DVE_SPLITS = (2, 4, 5, 6, 7), (0, 1, 3, 8)
    CHOICES_FIRST = TILES - 2
    LOOP = (FRONT + R, BEHIND - R)
    assert FRONT % R == 0 and ROUTED % R == 0 and KC == 2 and GROUPS == 4 and SLOTS >= ROUTED

    at, col = 0, {}
    for name, n in (("affT", C), ("condT", batches), ("affb", KC), ("bias", KC), ("gate", KC * E), ("WT", KC * C)):
        col[name] = slice(at, at + n)
        at += n
    SMALL = at
    HEAD = col["WT"].start

    y_rows = nc.dram_tensor("y_rows", (T, C), F32).ap()
    z_rows = nc.dram_tensor("z_rows", (TOP * T, C), F32).ap()

    with ExitStack() as ctx:
        def sb(name, shape, dt=F32):
            return ctx.enter_context(nc.sbuf_tensor(name, shape, dt))

        def sem(name):
            return ctx.enter_context(nc.semaphore(name))

        def sems(name, n):
            return [sem(f"{name}{i}") for i in range(n)]

        w_hi = sb("w_hi", [P, NF, KC, FFN_W], F32R)
        w_lo = sb("w_lo", [P, NF, KC, FFN_W], F32R)
        w_raw = sb("w_raw", [P, WB, KC, FFN_W])
        base = sb("base", [P, TILES, KC, P])
        base_rows = base[:, :, :, :].rearrange("p t k m -> p t (k m)")
        x_in_sb = sb("x_in_sb", [P, R, C])
        z_sb = sb("z_sb", [P, R, C])
        xT_s = sb("xT_s", [P, R, 2, KC, P], F32R)
        aT = sb("aT", [P, 2, KC, P], F32R)
        hidden = sb("hidden", [P, 2, R, F])
        z_in = w_raw[:, :, :, :].rearrange("p a k n -> p (a k n)")[:, 0:ZR * TOP * C].rearrange(
            "p (n c m) -> p n c m", n=ZR, c=TOP)
        ident = sb("ident", [P, P])
        ones = sb("ones", [P, 1])
        warm = sb("warm", [P, 1])
        rank = sb("rank", [P, TILES, E])
        below = sb("below", [P, P], BF16)
        ones_b = sb("ones_b", [P, P], BF16)
        member = sb("member", [P, TILES + 1, E], BF16)
        tiles_i = sb("tiles_i", [P, E // 2 + E], I32)
        escan = sb("escan", [P, 2, E // 2 + E])
        iota_row = sb("iota_row", [P, P, PAIRS], BF16)
        iota_slot = sb("iota_slot", [P, SLOTS, PAIRS], BF16)
        iota_map = sb("iota_map", [P, MAPPED])
        iota_pair = sb("iota_pair", [P, PAIRS], BF16)
        part = sb("part", [P, 1])
        slot_g = sb("slot_g", [P, SLOTS], U32)
        slot_s = sb("slot_s", [P, SLOTS], U32)
        less = sb("less", [P, TILES, E])
        prob = sb("prob", [P, TILES, E])
        tmp = sb("tmp", [P, TILES, E])
        hit = sb("hit", [P, TOP, TILES, E])
        stat = sb("stat", [P, 5, TILES])
        w_pair = sb("w_pair", [P, TOP, TILES])

        with ExitStack() as stage1:
            ws1 = lambda name, shape, dt=F32: stage1.enter_context(nc.sbuf_tensor(name, shape, dt))
            small_sb = ws1("small_sb", [P, SMALL])
            W_sq = ws1("W_sq", [P, KC, C])
            styles = ws1("styles", [P, KC, batches])
            styles_sq = ws1("styles_sq", [P, KC, batches])
            demod = ws1("demod", [P, KC, batches])
            dem = ws1("dem", [P, 3, KC, batches])
            x_raw = ws1("x_raw", [P, 2, KC, GT * P])
            x_mod = ws1("x_mod", [P, 2, KC, GT * P])
            y_row = ws1("y_row", [P, 2, GT, C])

        posh = sb("posh", [P, TOP, TILES, E])
        e_pair = sb("e_pair", [P, TOP, TILES])
        pos = sb("pos", [P, PAIRS])
        pos_i = sb("pos_i", [P, 3, PAIRS], I32)
        pos_lo = sb("pos_lo", [P, PAIRS], BF16)
        pos_hi = sb("pos_hi", [P, PAIRS], BF16)
        one_lo = sb("one_lo", [P, P, PAIRS], BF16)
        one_hi = sb("one_hi", [P, SLOTS, PAIRS], BF16)
        pay = sb("pay", [P, 2, SLOTS, PAIRS], BF16)
        slot_f = sb("slot_f", [P, 4, SLOTS])
        emap_c = sb("emap_c", [P, MAPPED, E])
        emap_f = sb("emap_f", [P, MAPPED])
        packs = sb("packs", [P, 2, TURNS])
        packs_i = sb("packs_i", [P, TURNS], I32)

        bank = [ctx.enter_context(nc.psum_tensor(f"bank{i}", [P, 512], F32)) for i in range(8)]
        gu = bank[0:R]
        t1_ps = bank[3][:, 0:C].rearrange("p (k m) -> p k m", k=KC)
        t2_ps = bank[4][:, 0:C].rearrange("p (k m) -> p k m", k=KC)
        z_ps = bank[5][:, 0:C]
        logit_bank = [bank[6], bank[7]]
        logit_ps = [b[:, 0:TILES * E].rearrange("p (t e) -> p t e", t=TILES) for b in logit_bank]
        misc_ps = bank[7]
        style_ps = misc_ps[:, 0:KC * batches].rearrange("p (k b) -> p k b", k=KC)
        demod_ps = misc_ps[:, KC * batches:2 * KC * batches].rearrange("p (k b) -> p k b", k=KC)
        BEFORE, SLOT_AT = 16, 16 + (TILES + 1) * E
        before_ps = misc_ps[:, BEFORE:SLOT_AT].rearrange("p (t e) -> p t e", e=E)
        slot_ps = misc_ps[:, SLOT_AT:SLOT_AT + 2 * SLOTS].rearrange("p (a s) -> p a s", a=2)
        y_ps = [[bank[0], bank[1]], [bank[2], bank[3]]]
        rows_ps = [bank[4], bank[5]]

        head_in = sem("head_in")
        W_in = sem("W_in")
        xT_in = [sems("xT_in_even", KC), sems("xT_in_odd", KC)]
        w_in = sems("w_in", WB)
        base_in = sems("base_in", R)
        consts = sem("consts")
        iotas = sem("iotas")
        style_mm = sem("style_mm")
        styles_done = sem("styles_done")
        W_sq_done = sem("W_sq_done")
        demod_mm = sem("demod_mm")
        demod_sqrt = sem("demod_sqrt")
        demod_done = sem("demod_done")
        x_scaled = sem("x_scaled")
        cond_mm = sem("cond_mm")
        y_biased = sem("y_biased")
        y_clipped = sem("y_clipped")
        rows_mm = sem("rows_mm")
        rows_copied = sem("rows_copied")
        y_stored = sems("y_stored", 2)
        logit_mm = sem("logit_mm")
        w_hi_done = sem("w_hi_done")
        w_lo_pool = sem("w_lo_pool")
        w_lo_dve = sem("w_lo_dve")
        rt = sem("rt")
        exp_ready = sem("exp_ready")
        exp_done = sem("exp_done")
        member_done = sem("member_done")
        before_mm = sem("before_mm")
        one_hot_done = sem("one_hot_done")
        slots_mm = sem("slots_mm")
        slots_done = sem("slots_done")
        emap_done = sem("emap_done")
        gathered = sems("gathered", R)
        t1_mm = sem("t1_mm")
        xT_hi_done = sem("xT_hi_done")
        shared_lo_done = sem("shared_lo_done")
        routed_lo_done = sem("routed_lo_done")
        gu_mm = sem("gu_mm")
        silu_done = sem("silu_done")
        product_done = sem("product_done")
        t2_mm = sem("t2_mm")
        aT_hi_done = sem("aT_hi_done")
        aT_lo_done = sem("aT_lo_done")
        down_mm = sem("down_mm")
        z_read = sem("z_read")
        z_out = sems("z_out", R)
        shared_added = sem("shared_added")
        z_back = sems("z_back", ZR)
        first_added = sem("first_added")
        both_added = sem("both_added")
        stored = sem("stored")

        f32 = lambda ap: ap.bitcast(F32)
        affT, condT, affb, biasT = (small_sb[:, col[n]] for n in ("affT", "condT", "affb", "bias"))
        WT = small_sb[:, col["WT"]].rearrange("p (k o) -> p k o", k=KC)
        gate_w = small_sb[:, col["gate"]].rearrange("p (k e) -> p k e", k=KC)
        x_rows_v = x_rows.rearrange("(n p) c -> p n c", p=P)
        out_v = out.rearrange("(n p) c -> p n c", p=P)
        y_v = y_rows.rearrange("(n p) c -> p n c", p=P)
        z_v = z_rows.rearrange("(a n p) c -> p n a c", p=P, a=TOP)
        PICKS = (slice(0, 2 * GT), slice(2 * GT, TILES))
        batch_of = lambda g: g // (GROUPS // batches)

        def routed(n):
            return not isinstance(n, int) or FRONT <= n < BEHIND

        def shared_tile(n):
            return n if n < FRONT else n - ROUTED

        def slot_tile(n):
            return n - FRONT

        def is_step(n):
            return not isinstance(n, int) or n < STEPS

        def walk(eng, iteration):
            for n in range(LOOP[0]):
                iteration(n, n % R, n // R)
            with eng.Fori(LOOP[0] // R, LOOP[1] // R) as turn:
                for j in range(R):
                    iteration(turn * R + j, j, turn)
            for n in range(LOOP[1], STEPS):
                iteration(n, n % R, n // R)

        def wait_split(eng, f):
            eng.wait_ge(w_lo_dve, sum(i <= f for i in DVE_SPLITS))
            if f >= POOL_SPLITS[0]:
                eng.wait_ge(w_lo_pool, sum(i <= f for i in POOL_SPLITS))

        block = ctx.enter_context(nc.Block())

        @block.sync
        def _(sp):
            def load_x(g):
                for k in range(KC):
                    if g >= 2:
                        sp.wait_ge(x_scaled, (g - 2) * KC + k + 1)
                    sp.dma_start(x_raw[:, g % 2, k, :], xT[g, k]).then_inc(xT_in[g % 2][k], 16)

            def load_w(f):
                if f >= WB:
                    sp.wait_ge(w_hi_done, f - WB + 1)
                    wait_split(sp, f - WB)
                sp.dma_start(w_raw[:, f % WB, :, :], ffn_w[f]).then_inc(w_in[f % WB], 16)

            def store_y(g):
                sp.wait_ge(rows_copied, 2 * g + 2)
                sp.dma_start(y_v[:, g * GT:(g + 1) * GT, :], y_row[:, g % 2, :, :]).then_inc(y_stored[g % 2], 16)

            sp.dma_start(small_sb[:, 0:HEAD], small[:, 0:HEAD]).then_inc(head_in, 16)
            sp.dma_start(small_sb[:, HEAD:SMALL], small[:, HEAD:SMALL]).then_inc(W_in, 16)
            load_x(0)
            load_x(1)
            load_w(0)
            load_x(2)
            load_w(1)
            load_x(3)
            for f in (2, 3, 4):
                load_w(f)
            for g in range(GROUPS):
                store_y(g)
                load_w(g + 5)
            for slot in range(R):
                sp.wait_ge(z_out[slot], 16 * (ROUTED // R))

            def load_z(t):
                if t >= ZR:
                    sp.wait_ge(both_added, t - ZR + 1)
                sp.dma_start(z_in[:, t % ZR, :, :], z_v[:, t, :, :]).then_inc(z_back[t % ZR], 16)

            def store(t):
                if t < CHOICES_FIRST:
                    sp.wait_ge(both_added, t + 1)
                else:
                    sp.wait_ge(shared_added, t + 1)
                sp.dma_start(out_v[:, t, :], base_rows[:, t, :]).then_inc(stored, 16)

            for t in range(ZR):
                load_z(t)
            for t in range(TILES):
                store(t)
                if t + ZR < TILES:
                    load_z(t + ZR)
            sp.wait_ge(stored, 16 * TILES)

        @block.gpsimd
        def _(pool):
            pool.memset(ones[:, :], 1.0)
            pool.memset(ident[:, :], 0.0).then_inc(consts, 1)
            pool.wait_ge(consts, 1)
            pool.affine_select(out=ident[:, :], in_=ident[:, :], compare_op=ALU.not_equal, fill=1.0,
                               base=0, pattern=[[-1, P]], channel_multiplier=1).then_inc(consts, 1)
            pool.wait_ge(W_in, 16)
            pool.tensor_tensor(W_sq[:, :, :], WT, WT, ALU.mult).then_inc(W_sq_done, 1)
            for e in range(E):
                pool.memset(rank[:, :, e:e + 1], float(E - e))
            pool.memset(ones_b[:, :], 1.0)
            pool.memset(member[:, TILES, :], 0.0)
            pool.memset(tiles_i[:, :], 0)
            pool.memset(escan[:, :, :], 0.0).then_inc(iotas, 1)
            pool.iota(iota_map[:, :], [[1, MAPPED]], base=0, channel_multiplier=0,
                      allow_small_or_imprecise_dtypes=True)
            pool.iota(iota_pair[:, :], [[1, PAIRS]], base=1, channel_multiplier=0,
                      allow_small_or_imprecise_dtypes=True)
            pool.iota(part[:, :], [[0, 1]], base=0, channel_multiplier=1,
                      allow_small_or_imprecise_dtypes=True)
            pool.wait_ge(iotas, 1)
            pool.affine_select(out=below[:, :], in_=ones_b[:, :], compare_op=ALU.is_gt, fill=0.0,
                               base=0, pattern=[[1, P]], channel_multiplier=-1).then_inc(iotas, 1)

            def split_w(f):
                pool.wait_ge(w_in[f % WB], 16 * (f // WB + 1))
                pool.wait_ge(w_hi_done, f + 1)
                pool.tensor_tensor(w_lo[:, f, :, :], w_raw[:, f % WB, :, :], f32(w_hi[:, f, :, :]),
                                   ALU.subtract).then_inc(w_lo_pool, 1)

            pool.iota(iota_slot[:, :, :], [[1, SLOTS], [0, PAIRS]], base=0, channel_multiplier=0,
                      allow_small_or_imprecise_dtypes=True).then_inc(iotas, 1)
            pool.iota(iota_row[:, :, :], [[1, P], [0, PAIRS]], base=0, channel_multiplier=0,
                      allow_small_or_imprecise_dtypes=True).then_inc(iotas, 1)
            split_w(2)
            split_w(4)

            def shared_lo(n):
                pool.wait_ge(xT_hi_done, n + 1)
                pool.tensor_tensor(xT_s[:, n % R, 1, :, :], base[:, shared_tile(n), :, :],
                                   f32(xT_s[:, n % R, 0, :, :]), ALU.subtract).then_inc(shared_lo_done, 1)

            def add_shared(n):
                t = shared_tile(n)
                pool.wait_ge(z_read, n + 1)
                if t < CHOICES_FIRST:
                    pool.wait_ge(base_in[t % R], 16 * (t // R + 1))
                else:
                    pool.wait_ge(both_added, t + 1)
                pool.tensor_tensor(base_rows[:, t, :], z_sb[:, n % R, :], base_rows[:, t, :],
                                   ALU.add).then_inc(shared_added, 1)

            def gather(n):
                r = slot_tile(n)
                if r >= R:
                    pool.wait_ge(t1_mm, r - R + 1)
                pool.indirect_dma_start(x_in_sb[:, n % R, :], None, y_rows,
                                        bass.IndirectOffsetOnAxis(ap=slot_g[:, r:r + 1], axis=0)
                                        ).then_inc(gathered[n % R], 16)

            def scatter(n):
                pool.wait_ge(z_read, n + 1)
                r = slot_tile(n)
                pool.indirect_dma_start(z_rows, bass.IndirectOffsetOnAxis(ap=slot_s[:, r:r + 1], axis=0),
                                        z_sb[:, n % R, :], None, bounds_check=TOP * T - 1,
                                        oob_is_err=False).then_inc(z_out[n % R], 16)

            for n in range(R):
                shared_lo(n)
            split_w(5)
            split_w(6)
            for n in range(STEPS):
                if is_step(n + 3) and not routed(n + 3):
                    shared_lo(n + 3)
                if n == INVERT + 1:
                    for m in range(FRONT + 1, FRONT + R):
                        gather(m)
                if n == 0:
                    split_w(7)
                if n == INVERT:
                    pool.wait_ge(slots_done, 1)
                    for slot in range(2):
                        pool.wait_ge(y_stored[slot], 16 * (GROUPS // 2))
                    gather(FRONT)
                if n + 2 * R < BEHIND and n >= FRONT:
                    gather(n + 2 * R)
                if routed(n):
                    scatter(n)
                else:
                    add_shared(n)
                if FRONT - R <= n < FRONT:
                    gather(n + 2 * R)
                if n == FRONT - 1:
                    pool.wait_ge(slots_done, 2)

        @block.scalar
        def _(act):
            act.wait_ge(consts, 1)
            act.activation(warm[:, :], ones[:, :], ACT.Sqrt)

            def split_w(f):
                act.wait_ge(w_in[f % WB], 16 * (f // WB + 1))
                act.copy(w_hi[:, f, :, :], w_raw[:, f % WB, :, :]).then_inc(w_hi_done, 1)

            def bias_y(g):
                for k in range(KC):
                    act.wait_ge(cond_mm, g * KC + k + 1)
                    act.activation(base[:, g * GT:(g + 1) * GT, k, :],
                                   y_ps[g % 2][k][:, :].rearrange("p (t m) -> p t m", t=GT), ACT.Identity,
                                   bias=biasT[:, k:k + 1],
                                   scale=demod[:, k, batch_of(g):batch_of(g) + 1]).then_inc(y_biased, 1)

            def copy_rows(g):
                if g >= 2:
                    act.wait_ge(y_stored[g % 2], 16 * (g // 2))
                for h in range(2):
                    act.wait_ge(rows_mm, 2 * g + h + 1)
                    act.copy(y_row[:, g % 2, 2 * h:2 * h + 2, :],
                             rows_ps[h][:, :].rearrange("p (t c) -> p t c", t=2)).then_inc(rows_copied, 1)

            act.wait_ge(demod_done, 1)
            act.activation(dem[:, 1, :, :], dem[:, 0, :, :], ACT.Sqrt).then_inc(demod_sqrt, 1)
            act.wait_ge(demod_done, 5)
            bias_y(0)
            split_w(0)
            split_w(1)
            bias_y(1)
            copy_rows(0)
            split_w(2)
            bias_y(2)
            split_w(3)
            copy_rows(1)
            split_w(4)
            bias_y(3)
            def xT_hi(n, slot):
                if routed(n):
                    act.wait_ge(t1_mm, slot_tile(n) + 1)
                    source = t1_ps
                else:
                    act.wait_ge(y_clipped, shared_tile(n) // GT + 1)
                    source = base[:, shared_tile(n), :, :]
                if not isinstance(n, int) or n >= R:
                    act.wait_ge(gu_mm, n - R + 1)
                act.copy(xT_s[:, slot, 0, :, :], source).then_inc(xT_hi_done, 1)

            def silu(n, slot):
                act.wait_ge(gu_mm, n + 1)
                if not isinstance(n, int) or n >= R:
                    act.wait_ge(product_done, n - R + 1)
                act.activation(hidden[:, 0, slot, :], gu[slot][:, 0:F], ACT.Silu).then_inc(silu_done, 1)

            def load_base(n):
                t = shared_tile(n)
                act.wait_ge(shared_lo_done, t + 1)
                if t >= R:
                    act.wait_ge(shared_added, t - R + 1)
                act.dma_start(base_rows[:, t, :], x_rows_v[:, t, :]).then_inc(base_in[t % R], 16)

            def aT_hi(n):
                act.wait_ge(t2_mm, n + 1)
                act.copy(aT[:, 0, :, :], t2_ps).then_inc(aT_hi_done, 1)

            def read_z(n, slot, turn):
                act.wait_ge(down_mm, n + 1)
                if not isinstance(n, int) or FRONT + R <= n < BEHIND + R:
                    act.wait_ge(z_out[slot], (turn - FRONT // R) * 16)
                elif n >= R:
                    act.wait_ge(shared_added, shared_tile(n - R) + 1)
                act.copy(z_sb[:, slot, :], z_ps).then_inc(z_read, 1)

            def iteration(n, slot, turn):
                aT_hi(n)
                if is_step(n + 3):
                    xT_hi(n + 3, slot)
                if is_step(n + 2):
                    silu(n + 2, (slot + 2) % R)
                if is_step(n + 2) and not routed(n + 2):
                    load_base(n + 2)
                if isinstance(n, int) and n == 0:
                    act.wait_ge(exp_ready, len(PICKS))
                    act.activation(prob[:, :, :], less[:, :, :], ACT.Exp).then_inc(exp_done, 1)
                if isinstance(n, int) and n == 0:
                    split_w(7)
                    split_w(8)
                read_z(n, slot, turn)

            for n in range(R):
                xT_hi(n, n)
            copy_rows(2)
            split_w(5)
            copy_rows(3)
            silu(0, 0)
            silu(1, 1)
            split_w(6)
            load_base(0)
            load_base(1)
            walk(act, iteration)

        @block.vector
        def _(dve):
            count = [0]

            def link(ins):
                count[0] += 1
                ins.then_inc(rt, 1)
                dve.wait_ge(rt, count[0])

            def scale_x(g):
                for k in range(KC):
                    dve.wait_ge(xT_in[g % 2][k], 16 * (g // 2 + 1))
                    if g >= 2:
                        dve.wait_ge(cond_mm, (g - 1) * KC)
                    dve.tensor_scalar(x_mod[:, g % 2, k, :], x_raw[:, g % 2, k, :],
                                      styles[:, k, batch_of(g):batch_of(g) + 1], None,
                                      ALU.mult).then_inc(x_scaled, 1)

            def clip_y(g):
                dve.wait_ge(y_biased, (g + 1) * KC)
                dve.tensor_scalar(base[:, g * GT:(g + 1) * GT, :, :], base[:, g * GT:(g + 1) * GT, :, :],
                                  CLAMP, -CLAMP, ALU.min, ALU.max).then_inc(y_clipped, 1)

            def split_w(f):
                dve.wait_ge(w_in[f % WB], 16 * (f // WB + 1))
                dve.wait_ge(w_hi_done, f + 1)
                dve.tensor_tensor(w_lo[:, f, :, :], w_raw[:, f % WB, :, :], f32(w_hi[:, f, :, :]),
                                  ALU.subtract).then_inc(w_lo_dve, 1)

            dve.wait_ge(head_in, 16)
            dve.wait_ge(style_mm, 1)
            for k in range(KC):
                ins = dve.tensor_scalar(styles[:, k, :], style_ps[:, k, :], GAIN, affb[:, k:k + 1],
                                        ALU.mult, ALU.add)
            link(ins)
            dve.tensor_tensor(styles_sq[:, :, :], styles[:, :, :], styles[:, :, :], ALU.mult).then_inc(styles_done, 1)
            scale_x(0)
            scale_x(1)
            v, root, c = (dem[:, i, :, :] for i in range(3))
            dve.wait_ge(demod_mm, 1)
            dve.tensor_scalar(v, demod_ps, DEMOD_EPS, None, ALU.add).then_inc(demod_done, 1)
            dve.wait_ge(demod_sqrt, 1)
            dve.reciprocal(demod[:, :, :], root).then_inc(demod_done, 1)
            dve.wait_ge(demod_done, 2)
            dve.tensor_tensor(c, demod[:, :, :], demod[:, :, :], ALU.mult).then_inc(demod_done, 1)
            dve.wait_ge(demod_done, 3)
            dve.scalar_tensor_tensor(out=c, in0=c, scalar=-0.5, in1=v, op0=ALU.mult, op1=ALU.mult).then_inc(demod_done, 1)
            dve.wait_ge(demod_done, 4)
            dve.scalar_tensor_tensor(out=demod[:, :, :], in0=c, scalar=1.5, in1=demod[:, :, :],
                                     op0=ALU.add, op1=ALU.mult).then_inc(demod_done, 1)
            def pick(tiles):
                n = tiles.stop - tiles.start
                bc = lambda m: m.unsqueeze(2).broadcast_to([P, n, E])
                mx, second, key = (stat[:, i, tiles] for i in range(3))
                first_hit, second_hit = hit[:, 0, tiles, :], hit[:, 1, tiles, :]
                under, others, ranks = less[:, tiles, :], tmp[:, tiles, :], rank[:, tiles, :]

                def lowest(h):
                    link(dve.tensor_reduce(key, h, AX_X, ALU.max))
                    link(dve.tensor_tensor(h, h, bc(key), ALU.is_equal))

                dve.wait_ge(logit_mm, tiles.stop // GT)
                link(dve.tensor_reduce(mx, logit_ps[PICKS.index(tiles)][:, tiles, :], AX_X, ALU.max))
                dve.tensor_tensor(under, logit_ps[PICKS.index(tiles)][:, tiles, :], bc(mx), ALU.subtract).then_inc(exp_ready, 1)
                dve.wait_ge(exp_ready, PICKS.index(tiles) + 1)
                link(dve.scalar_tensor_tensor(out=first_hit, in0=under, scalar=0.0, in1=ranks,
                                              op0=ALU.is_equal, op1=ALU.mult))
                lowest(first_hit)
                link(dve.scalar_tensor_tensor(out=others, in0=first_hit, scalar=FAR_BELOW, in1=under,
                                              op0=ALU.mult, op1=ALU.add))
                link(dve.tensor_reduce(second, others, AX_X, ALU.max))
                link(dve.tensor_tensor(second_hit, others, bc(second), ALU.is_equal))
                link(dve.tensor_tensor(second_hit, second_hit, ranks, ALU.mult))
                lowest(second_hit)
                dve.tensor_tensor(member[:, tiles, :], first_hit, second_hit, ALU.add).then_inc(member_done, 1)

            over_pairs = lambda m: m.rearrange("p t e -> p (t e)").unsqueeze(1).broadcast_to([P, TOP, TILES * E])
            hit_flat = hit[:, :, :, :].rearrange("p a t e -> p a (t e)")

            total, rsum = stat[:, 3, :], stat[:, 4, :]

            def choice_probabilities():
                dve.wait_ge(exp_done, 1)
                dve.tensor_reduce(total, prob[:, :, :], AX_X, ALU.add)
                link(dve.tensor_tensor(posh[:, :, :, :].rearrange("p a t e -> p a (t e)"), hit_flat,
                                       over_pairs(prob[:, :, :]), ALU.mult))
                link(dve.tensor_reduce(e_pair[:, :, :].rearrange("p a t -> p (a t)"),
                                       posh[:, :, :, :].rearrange("p a t e -> p (a t) e"), AX_X, ALU.add))

            def pair_weights():
                link(dve.tensor_tensor(rsum, e_pair[:, 0, :], e_pair[:, 1, :], ALU.add))
                link(dve.scalar_tensor_tensor(out=rsum, in0=total, scalar=TOPW_EPS, in1=rsum,
                                              op0=ALU.mult, op1=ALU.add))
                link(dve.reciprocal(rsum, rsum))
                link(dve.tensor_tensor(w_pair[:, :, :], e_pair[:, :, :],
                                       rsum.unsqueeze(1).broadcast_to([P, TOP, TILES]), ALU.mult))

            def positions():
                H = E // 2
                dve.wait_ge(before_mm, 1)
                link(dve.tensor_scalar(tiles_i[:, H:], before_ps[:, TILES, :], float(P - 1), None, ALU.add))
                link(dve.tensor_scalar(tiles_i[:, H:], tiles_i[:, H:], 7, None, ALU.logical_shift_right))
                link(dve.tensor_tensor(escan[:, 0, H:], tiles_i[:, H:], tiles_i[:, H - 1:H + E - 1], ALU.add))
                es = 0
                for d in (2, 4):
                    link(dve.tensor_tensor(escan[:, 1 - es, H:], escan[:, es, H:], escan[:, es, H - d:H + E - d], ALU.add))
                    es = 1 - es
                first_tile = escan[:, es, H - 1:H + E - 1]
                link(dve.scalar_tensor_tensor(out=tmp[:, :, :], in0=first_tile.unsqueeze(1).broadcast_to([P, TILES, E]),
                                              scalar=float(P), in1=before_ps[:, 0:TILES, :], op0=ALU.mult, op1=ALU.add))
                link(dve.tensor_tensor(posh[:, :, :, :].rearrange("p a t e -> p a (t e)"), hit_flat,
                                       over_pairs(tmp[:, :, :]), ALU.mult))
                link(dve.tensor_reduce(pos[:, :], posh[:, :, :, :].rearrange("p a t e -> p (a t) e"), AX_X, ALU.add))
                link(dve.tensor_copy(pos_i[:, 0, :], pos[:, :]))
                dve.tensor_scalar(pos_i[:, 1, :], pos_i[:, 0, :], P - 1, None, ALU.bitwise_and)
                link(dve.tensor_scalar(pos_i[:, 2, :], pos_i[:, 0, :], 7, None, ALU.logical_shift_right))
                dve.tensor_copy(pos_lo[:, :], pos_i[:, 1, :])
                link(dve.tensor_copy(pos_hi[:, :], pos_i[:, 2, :]))
                return es

            over_slots = lambda m: m.unsqueeze(1).broadcast_to([P, SLOTS, PAIRS])

            def one_hot_tiles():
                link(dve.tensor_tensor(one_hi[:, :, :], iota_slot[:, :, :], over_slots(pos_hi[:, :]), ALU.is_equal))
                dve.tensor_tensor(pay[:, 0, :, :], one_hi[:, :, :], over_slots(iota_pair[:, :]), ALU.mult).then_inc(one_hot_done, 1)
                dve.tensor_scalar(pay[:, 1, :, :], one_hi[:, :, :], part[:, 0:1], None, ALU.mult).then_inc(one_hot_done, 1)

            def one_hot_rows(a, b):
                dve.tensor_tensor(one_lo[:, :, a:b], iota_row[:, :, a:b],
                                  pos_lo[:, a:b].unsqueeze(1).broadcast_to([P, P, b - a]),
                                  ALU.is_equal).then_inc(one_hot_done, 1)

            def slot_indices():
                for slot in range(2):
                    dve.wait_ge(y_stored[slot], 16 * (GROUPS // 2))
                dve.wait_ge(slots_mm, 1)
                link(dve.tensor_copy(slot_f[:, 1, :], slot_ps[:, 1, :]))
                link(dve.scalar_tensor_tensor(out=slot_f[:, 0, :], in0=slot_ps[:, 0, :], scalar=float(P),
                                              in1=slot_f[:, 1, :], op0=ALU.mult, op1=ALU.add))
                link(dve.tensor_scalar(slot_f[:, 2, :], slot_f[:, 0, :], float(T + P), float(-T), ALU.is_ge, ALU.mult))
                link(dve.scalar_tensor_tensor(out=slot_f[:, 2, :], in0=slot_f[:, 0, :], scalar=float(-P),
                                              in1=slot_f[:, 2, :], op0=ALU.add, op1=ALU.add))
                dve.tensor_scalar(slot_g[:, :], slot_f[:, 2, :], 0.0, None, ALU.max).then_inc(slots_done, 1)
                link(dve.tensor_scalar(slot_f[:, 3, :], slot_f[:, 0, :], float(P), OUT_OF_RANGE, ALU.is_lt, ALU.mult))
                dve.scalar_tensor_tensor(out=slot_s[:, :], in0=slot_f[:, 0, :], scalar=float(-P),
                                         in1=slot_f[:, 3, :], op0=ALU.add, op1=ALU.add).then_inc(slots_done, 1)

            def expert_map(es):
                H = E // 2
                link(dve.tensor_tensor(emap_c[:, :, :], iota_map[:, :].unsqueeze(2).broadcast_to([P, MAPPED, E]),
                                       escan[:, es, H:].unsqueeze(1).broadcast_to([P, MAPPED, E]), ALU.is_ge))
                link(dve.tensor_reduce(emap_f[:, :], emap_c[:, :, :], AX_X, ALU.add))
                link(dve.tensor_scalar(emap_f[:, :], emap_f[:, :], float(E - 1), 1.0, ALU.min, ALU.add))
                at_step = lambda j: emap_f[:, (j // R) * R:(j // R) * R + ROUTED].rearrange(
                    "p (t r) -> p t r", r=R)[:, :, j % R]
                link(dve.scalar_tensor_tensor(out=packs[:, 0, :], in0=at_step(4), scalar=16.0, in1=at_step(3),
                                              op0=ALU.mult, op1=ALU.add))
                link(dve.scalar_tensor_tensor(out=packs[:, 1, :], in0=packs[:, 0, :], scalar=16.0, in1=at_step(2),
                                              op0=ALU.mult, op1=ALU.add))
                link(dve.scalar_tensor_tensor(out=packs[:, 0, :], in0=packs[:, 1, :], scalar=16.0, in1=at_step(1),
                                              op0=ALU.mult, op1=ALU.add))
                dve.scalar_tensor_tensor(out=packs_i[:, :], in0=packs[:, 0, :], scalar=16.0, in1=at_step(0),
                                         op0=ALU.mult, op1=ALU.add).then_inc(emap_done, 1)

            def xT_lo(n, slot):
                dve.wait_ge(xT_hi_done, n + 1)
                dve.tensor_tensor(xT_s[:, slot, 1, :, :], t1_ps, f32(xT_s[:, slot, 0, :, :]),
                                  ALU.subtract).then_inc(routed_lo_done, 1)

            def product(n, slot):
                dve.wait_ge(silu_done, n + 1)
                dve.tensor_tensor(hidden[:, 1, slot, :], gu[slot][:, F:2 * F], hidden[:, 0, slot, :],
                                  ALU.mult).then_inc(product_done, 1)

            def aT_lo(n):
                dve.wait_ge(aT_hi_done, n + 1)
                dve.tensor_tensor(aT[:, 1, :, :], t2_ps, f32(aT[:, 0, :, :]), ALU.subtract).then_inc(aT_lo_done, 1)

            def add_choices(tiles):
                for choice, done in ((0, first_added), (1, both_added)):
                    for t in tiles:
                        if choice == 0:
                            dve.wait_ge(z_back[t % ZR], 16 * (t // ZR + 1))
                            if t < CHOICES_FIRST:
                                dve.wait_ge(shared_added, t + 1)
                            else:
                                dve.wait_ge(base_in[t % R], 16 * (t // R + 1))
                        else:
                            dve.wait_ge(first_added, t + 1)
                        dve.scalar_tensor_tensor(out=base_rows[:, t, :], in0=z_in[:, t % ZR, choice, :],
                                                 scalar=w_pair[:, choice, t:t + 1], in1=base_rows[:, t, :],
                                                 op0=ALU.mult, op1=ALU.add).then_inc(done, 1)

            def routing(n):
                if n == 0:
                    one_hot_tiles()
                    one_hot_rows(0, PAIRS // 2)
                    one_hot_rows(PAIRS // 2, PAIRS)
                elif n == INVERT:
                    slot_indices()
                    split_w(8)
                elif n == INVERT + 1:
                    expert_map(es)
                elif n == FRONT - 1:
                    choice_probabilities()
                elif n == FRONT + 1:
                    pair_weights()

            def iteration(n, slot, turn):
                aT_lo(n)
                if is_step(n + 3) and routed(n + 3):
                    xT_lo(n + 3, slot)
                if is_step(n + 2):
                    product(n + 2, (slot + 2) % R)
                if isinstance(n, int):
                    routing(n)
                if isinstance(n, int) and n >= ADDS_FROM:
                    add_choices(range(2 * (n - ADDS_FROM), 2 * (n - ADDS_FROM) + 2))

            clip_y(0)
            scale_x(2)
            split_w(0)
            split_w(1)
            scale_x(3)
            clip_y(1)
            clip_y(2)
            split_w(3)
            dve.wait_ge(iotas, 4)
            pick(PICKS[0])
            clip_y(3)
            pick(PICKS[1])
            product(0, 0)
            product(1, 1)
            es = positions()
            walk(dve, iteration)
            for t in range(2 * (STEPS - ADDS_FROM), TILES, 2):
                add_choices(range(t, t + 2))

        @block.tensor
        def _(pe):
            def three_pass(out_ap, s_hi, s_lo, m_hi, m_lo, first, last):
                pe.matmul(out_ap, s_hi, m_hi, start=first, stop=False)
                pe.matmul(out_ap, s_hi, m_lo, start=False, stop=False)
                return pe.matmul(out_ap, s_lo, m_hi, start=False, stop=last)

            pe.wait_ge(head_in, 16)
            for k in range(KC):
                ins = pe.matmul(style_ps[:, k, :], affT[:, k * P:(k + 1) * P], condT, start=True, stop=True)
            ins.then_inc(style_mm, 1)

            def demod_sums():
                pe.wait_ge(W_sq_done, 1)
                pe.wait_ge(styles_done, 1)
                for o in range(KC):
                    for k in range(KC):
                        ins = pe.matmul(demod_ps[:, o, :], W_sq[:, k, o * P:(o + 1) * P], styles_sq[:, k, :],
                                        start=(k == 0), stop=(k == KC - 1))
                ins.then_inc(demod_mm, 1)

            def cond(g):
                for o in range(KC):
                    if g >= 2:
                        pe.wait_ge(y_biased, (g - 2) * KC + o + 1)
                    for k in range(KC):
                        pe.wait_ge(x_scaled, g * KC + k + 1)
                        ins = pe.matmul(y_ps[g % 2][o][:, :], WT[:, k, o * P:(o + 1) * P], x_mod[:, g % 2, k, :],
                                        start=(k == 0), stop=(k == KC - 1))
                    ins.then_inc(cond_mm, 1)

            def rows(g):
                for h in range(2):
                    if g >= 1:
                        pe.wait_ge(rows_copied, 2 * (g - 1) + h + 1)
                    for j in range(2):
                        for k in range(KC):
                            ins = pe.transpose(rows_ps[h][:, j * C + k * P:j * C + (k + 1) * P],
                                               base[:, g * GT + 2 * h + j, k, :], ident[:, :])
                    ins.then_inc(rows_mm, 1)

            def logits(g):
                which = [g * GT < tiles.stop for tiles in PICKS].index(True)
                pe.wait_ge(y_clipped, g + 1)
                for t in range(g * GT, (g + 1) * GT):
                    for k in range(KC):
                        ins = pe.matmul(logit_bank[which][:, t * E:(t + WIDE) * E].rearrange("p (t e) -> p t e", t=WIDE),
                                        base[:, t, k, :], gate_w[:, k, :].unsqueeze(1).broadcast_to([P, WIDE, E]),
                                        start=(k == 0), stop=(k == KC - 1))
                ins.then_inc(logit_mm, 1)

            pe.wait_ge(W_in, 16)
            cond(0)
            demod_sums()
            pe.wait_ge(consts, 2)
            cond(1)
            for g in range(GROUPS):
                logits(g)
                rows(g)
                if g + 2 < GROUPS:
                    cond(g + 2)

            def t1(n, slot, turn):
                pe.wait_ge(gathered[slot], (turn - FRONT // R + 1) * 16)
                if not isinstance(n, int) or n > FRONT:
                    pe.wait_ge(routed_lo_done, slot_tile(n))
                for k in range(KC):
                    ins = pe.transpose(t1_ps[:, k, :], x_in_sb[:, slot, k * P:(k + 1) * P], ident[:, :])
                ins.then_inc(t1_mm, 1)

            pack = pe.alloc_register("expert_pack")

            def load_pack(routed_turn):
                pe.reg_load(pack, packs_i[0:1, bass.ds(routed_turn, 1)])

            def unpack():
                word = pe.snap(pack)
                return [nc.s_assert_within(pe.snap((word >> (4 * j)) & 15), 1, E,
                                          skip_runtime_bounds_check_because="expert_map() bounds them to 1..E")
                        for j in range(R + 2)]

            def gate_up(n, slot, f):
                if routed(n):
                    pe.wait_ge(routed_lo_done, slot_tile(n) + 1)
                else:
                    pe.wait_ge(shared_lo_done, shared_tile(n) + 1)
                if not isinstance(n, int) or n >= R:
                    pe.wait_ge(product_done, n - R + 1)
                for k in range(KC):
                    ins = three_pass(gu[slot][:, :].unsqueeze(1), xT_s[:, slot, 0, k, :], xT_s[:, slot, 1, k, :],
                                     w_hi[:, bass.ds(f, 1), k, 0:2 * F], w_lo[:, bass.ds(f, 1), k, 0:2 * F],
                                     k == 0, k == KC - 1)
                ins.then_inc(gu_mm, 1)

            def t2(n, slot):
                pe.wait_ge(product_done, n + 1)
                if not isinstance(n, int) or n >= 1:
                    pe.wait_ge(aT_lo_done, n)
                for k in range(KC):
                    ins = pe.transpose(t2_ps[:, k, :], hidden[:, 1, slot, k * P:(k + 1) * P], ident[:, :])
                ins.then_inc(t2_mm, 1)

            def down(n, f):
                pe.wait_ge(aT_lo_done, n + 1)
                if not isinstance(n, int) or n >= 1:
                    pe.wait_ge(z_read, n)
                for k in range(KC):
                    ins = three_pass(z_ps.unsqueeze(1), aT[:, 0, k, :], aT[:, 1, k, :],
                                     w_hi[:, bass.ds(f, 1), k, 2 * F:FFN_W], w_lo[:, bass.ds(f, 1), k, 2 * F:FFN_W],
                                     k == 0, k == KC - 1)
                ins.then_inc(down_mm, 1)

            def prefixes():
                pe.wait_ge(member_done, len(PICKS))
                pe.matmul(before_ps, below[:, :], member[:, :, :], start=True, stop=False)
                for t in range(TILES):
                    behind = TILES - t
                    ins = pe.matmul(before_ps[:, t + 1:TILES + 1, :], ones_b[:, :],
                                    member[:, t, :].unsqueeze(1).broadcast_to([P, behind, E]),
                                    start=False, stop=(t == TILES - 1))
                ins.then_inc(before_mm, 1)

            def invert():
                for q in range(PAIRS):
                    if q % (PAIRS // 2) == 0:
                        pe.wait_ge(one_hot_done, 3 if q == 0 else 4)
                    ins = pe.matmul(slot_ps, one_lo[:, :, q], pay[:, :, :, q],
                                    start=(q == 0), stop=(q == PAIRS - 1))
                ins.then_inc(slots_mm, 1)

            def iteration(n, slot, turn, experts):
                t2(n, slot)
                if is_step(n + 3) and routed(n + 3):
                    t1(n + 3, slot, turn + 1)
                if is_step(n + 2):
                    gate_up(n + 2, (slot + 2) % R, experts[slot + 2])
                if slot == 0 and routed(n) and (not isinstance(n, int) or n + R < FRONT + ROUTED):
                    load_pack(turn - FRONT // R + 1)
                if isinstance(n, int) and n == INVERT:
                    invert()
                down(n, experts[slot])

            def shared_turn(turn):
                experts = [0] * (R + 2)
                for j in range(R):
                    if turn * R + j == FRONT - 2:
                        wait_split(pe, NF - 1)
                        pe.wait_ge(emap_done, 1)
                        load_pack(0)
                        experts[R:] = unpack()[0:2]
                    if turn * R + j < STEPS:
                        iteration(turn * R + j, j, turn, experts)

            wait_split(pe, 0)
            gate_up(0, 0, 0)
            gate_up(1, 1, 0)
            prefixes()
            pe.wait_ge(rows_copied, 2 * GROUPS)
            routed_from, routed_to = FRONT // R, BEHIND // R
            for n in range(FRONT - R):
                iteration(n, n % R, n // R, [0] * (R + 2))
            shared_turn(routed_from - 1)
            experts = unpack()
            for j in range(R):
                iteration(FRONT + j, j, routed_from, experts)
            with pe.Fori(routed_from + 1, routed_to - 1) as turn:
                experts = unpack()
                for j in range(R):
                    iteration(turn * R + j, j, turn, experts)
            experts = unpack()[0:R] + [0, 0]
            for j in range(R):
                iteration((routed_to - 1) * R + j, j, routed_to - 1, experts)
            for turn in range(routed_to, -(-STEPS // R)):
                shared_turn(turn)


_OUT = "out_dram"


def kernel(**inputs):
    import numpy as np
    import concourse.bacc as bacc
    from concourse.bass_utils import run_bass_kernel_spmd

    a = {k: np.asarray(v) for k, v in inputs.items()}
    x = a["x"]
    B, L, C = x.shape
    E = a["L0_ffn_gate_w"].shape[1]
    chunks = lambda m: m.reshape(C // P, P, -1).transpose(1, 0, 2).reshape(P, -1)
    small = np.concatenate([a["L0_cond_affine_w"].T, a["cond_512"].T, chunks(a["L0_cond_affine_b"]),
                            chunks(a["L0_cond_bias"]), chunks(a["L0_ffn_gate_w"]), chunks(a["L0_cond_weight"].T)], axis=1)
    both = lambda n: np.concatenate([a["L0_ffn_sw_" + n][None], a["L0_ffn_ew_" + n]], axis=0)
    ffn = np.concatenate([both("gate"), both("up"), both("down")], axis=2)
    ffn = ffn.reshape(E + 1, C // P, P, ffn.shape[2]).transpose(0, 2, 1, 3)
    arrays = {"xT": x.reshape(-1, GROUP_TOKENS, C // P, P).transpose(0, 2, 3, 1), "x_rows": x.reshape(B * L, C),
              "small": small, "ffn_w": ffn}
    arrays = {n: np.ascontiguousarray(v) for n, v in arrays.items()}

    nc = bacc.Bacc("TRN2", target_bir_lowering=False, num_devices=1)
    aps = {n: nc.dram_tensor(n, v.shape, mybir.dt.from_np(v.dtype), kind="ExternalInput").ap()
           for n, v in arrays.items()}
    out = nc.dram_tensor(_OUT, (B * L, C), F32, kind="ExternalOutput").ap()
    adaln_moe_ffn(nc, out=out, batches=B, n_experts=E, **aps)
    r = run_bass_kernel_spmd(nc, [arrays], core_ids=[0])
    return r.results[0][_OUT].reshape(B, L, C)
```
